# Optimizing a Trainium2 kernel written in Bass

```python
import numpy as np
import jax
import jax.numpy as jnp

def _softmax(x, axis=-1):
    return jax.nn.softmax(x, axis=axis)
def _gelu(x):
    return jax.nn.gelu(x, approximate=True)
def _silu(x):
    return jax.nn.silu(x)
def _sigmoid(x):
    return jax.nn.sigmoid(x)
def _layernorm(x, axis=-1, eps=1e-5):
    m = jnp.mean(x, axis=axis, keepdims=True)
    v = jnp.var(x, axis=axis, keepdims=True)
    return (x - m) / jnp.sqrt(v + eps)
def _scatter_add(tgt, idx, src, axis=0):
    return tgt.at[idx].add(src)
def _segment_sum(src, seg, n):
    return jax.ops.segment_sum(src, seg, n)

kernel_name = 'mk_adj_seq_d1_adj_128_027991'

def setup_inputs(seed: int = 0):
    np.random.seed(seed)
    _w = jnp.asarray
    def _rec_inputs():
        import jax
        import jax.numpy as jnp
        _gk = jax.random.key(seed)
        x = -0.003407 + 1.001 * jax.random.normal(jax.random.fold_in(_gk, 1), (3327, 128), jnp.float32)
        _a = jax.random.bernoulli(jax.random.fold_in(_gk, 2), 0.00120228, (3327, 3327))
        adj = _a.astype(jnp.int32)
        return x, adj
    x, adj = _rec_inputs()
    def _L0_gnn_setup():
        import jax, jax.numpy as jnp
        import numpy as np
        LAYER_IDX = 2
        T = 5
        K = 2
        EXP_DILATION = False
        QUANTILES = (0.25, 0.5, 0.75)
        SELF_RATIO = 0.5
        USE_SELF = True
        RESIDUAL = True
        key = jax.random.key(seed)
        kx, ka, kw = jax.random.split(key, 3)
        N, D = (1024, 128)
        x = jax.random.normal(kx, (N, D), dtype=jnp.float32)
        A = (jax.random.uniform(ka, (N, N)) < 0.05).astype(jnp.int32)
        W = jax.random.normal(kw, (D, D), dtype=jnp.float32) / np.sqrt(D).astype(np.float32)
        b = jnp.zeros((D,), dtype=jnp.float32)
        return {'x': x, 'A': A, 'W': W, 'b': b}
    _L0_gnn_all = _L0_gnn_setup()
    _L0_gnn_in = {k: v for k, v in _L0_gnn_all.items() if k in ('W', 'b', )}
    del _L0_gnn_all

    return {
        "x": x,
        "adj": adj,
        "L0_gnn_W": _L0_gnn_in["W"],
        "L0_gnn_b": _L0_gnn_in["b"],
    }

def reference(x, adj, L0_gnn_W, L0_gnn_b):
    import jax
    import jax.numpy as jnp
    def _L0_gnn_ref(x, A, W, b):
        import jax, jax.numpy as jnp
        import numpy as np
        LAYER_IDX = 2
        T = 5
        K = 2
        EXP_DILATION = False
        QUANTILES = (0.25, 0.5, 0.75)
        SELF_RATIO = 0.5
        USE_SELF = True
        RESIDUAL = True
        N, D = x.shape
        mask = A != 0
        rank = jnp.cumsum(mask.astype(jnp.int32), axis=1) - 1
        num_nbr = mask.sum(axis=1)
        m_i = jnp.where(num_nbr > T, jnp.ceil(num_nbr / K).astype(jnp.int32), jnp.int32(1))
        skip = m_i * (2 ** (LAYER_IDX - 1) if EXP_DILATION else 1)
        remove = mask & ((rank + 1) % skip[:, None] == 0)
        keep = mask & ~remove
        n_keep = keep.sum(axis=1)
        big = jnp.finfo(x.dtype).max
        vals = jnp.where(keep[:, :, None], x[None, :, :], big)
        svals = jnp.sort(vals, axis=1)
        w_q = jnp.asarray(1.0 / len(QUANTILES), x.dtype)
        agg = jnp.zeros((N, D), x.dtype)
        for q in QUANTILES:
            idx = jnp.maximum(jnp.ceil(q * n_keep).astype(jnp.int32) - 1, 0)
            picked = jnp.take_along_axis(svals, idx[:, None, None], axis=1)[:, 0, :]
            agg = agg + w_q * picked
        agg = jnp.where((n_keep > 0)[:, None], agg, jnp.zeros((), x.dtype))
        if USE_SELF:
            agg = (1.0 - SELF_RATIO) * agg + SELF_RATIO * x
        out = agg @ W.T + b
        if RESIDUAL:
            out = out + x
        return out

    x = _L0_gnn_ref(x, adj, L0_gnn_W, L0_gnn_b)
    return x


_drawn_inputs = setup_inputs


def setup_inputs(seed=0):
    import zlib

    import numpy as np

    out = dict(_drawn_inputs(seed))
    spreads = {'L0_gnn_b': (0.0, 0.1)}
    factors = {}
    for name, (base, spread) in spreads.items():
        noise = np.random.default_rng([zlib.crc32(name.encode()), seed]).standard_normal(out[name].shape)
        drawn = base * np.exp(spread * noise) if base else spread * noise
        out[name] = jnp.asarray(drawn.astype(out[name].dtype))
    for name, factor in factors.items():
        out[name] = (out[name] * factor).astype(out[name].dtype)
    return out
```

```python
from contextlib import ExitStack

import concourse.bass as bass
import numpy as np
from concourse import mybir

F32 = mybir.dt.float32
BF16 = mybir.dt.bfloat16
I32 = mybir.dt.int32
U32 = mybir.dt.uint32
ALU = mybir.AluOpType
ACT = mybir.ActivationFunctionType
AX = mybir.AxisListType

P = 128
GT = 6
RING = 3
CHUNK = 3
BITS = 16
TOP = 16
LEVELS = 3
SLOTS = 12
MID = 32
BIG = float(np.finfo(np.float32).max)
NOROW = 8192
THIRD_HALF = float(np.float32(0.5) * np.float32(1.0 / 3.0))
EXPONENT = 0x7F800000


def build(nc, x, adj, W, b, flag_rows, out):
    N, D = x.shape
    assert D == P
    NW = -(-N // BITS)
    assert NW <= 256 and 8 + BITS <= 24
    NP = NW * BITS
    NT = -(-N // P)
    LAST = N - P
    NG = NT // GT
    TT = NT - NG * GT
    assert 0 < TT <= CHUNK and GT % CHUNK == 0 and GT % RING == 0 and NG >= 2
    NC = GT // CHUNK

    with ExitStack() as ctx:
        def sb(name, shape, dt):
            return ctx.enter_context(nc.sbuf_tensor(name, shape, dt))

        def psum(name, shape):
            return ctx.enter_context(nc.psum_tensor(name, shape, F32))

        def sem(name):
            return ctx.enter_context(nc.semaphore(name))

        adj_ring = [sb(f"adj{i}", [P, NP], I32) for i in range(RING)]
        mask_ring = sb("mask_ring", [P, RING, NP], BF16)
        x_grp = sb("x_grp", [P, GT, D], F32)
        w_in = sb("w_in", [P, D], F32)
        wT = sb("wT", [P, D], F32)
        b_row = sb("b_row", [1, D], F32)
        b_col = sb("b_col", [P, 1], F32)
        ident = sb("ident", [P, P], F32)
        half_ident = sb("half_ident", [P, P], F32)
        ident_bf = sb("ident_bf", [P, P], BF16)
        bit_diag = sb("bit_diag", [P, BITS, P], BF16)
        before = sb("before", [P, P], BF16)
        ones_bf = sb("ones_bf", [P, P], BF16)
        ones_f = sb("ones_f", [P, P], F32)
        word_no = sb("word_no", [1, NW], BF16)
        dest_no = sb("dest_no", [P, P], F32)
        slot_no = sb("slot_no", [P, TOP], F32)
        row_code = sb("row_code", [P, NT], F32)
        counts_here = sb("counts_here", [P, NT], F32)
        pads = sb("pads", [P, 2, D], F32)
        col_no = sb("col_no", [P, NP], F32)
        spread = sb("spread", [MID, 2, P], F32)
        own_slot = sb("own_slot", [P, 8], F32)
        mid_pads = sb("mid_pads", [P, D], F32)
        part_i = sb("part_i", [P, 1], I32)
        part_a = sb("part_a", [P, 1], I32)
        part_f = sb("part_f", [P, 2], F32)
        sign_f = sb("sign_f", [P, 1], F32)
        rest_words = sb("rest_words", [P, NW], F32)
        words = sb("words", [P, GT, TOP], F32)
        words_i = sb("words_i", [P, GT, TOP], I32)
        low_i = sb("low_i", [P, GT, TOP], I32)
        col_base = sb("col_base", [P, GT, TOP], F32)
        rest = sb("rest", [P, GT, TOP], F32)
        high_bit = sb("high_bit", [P, GT, TOP], F32)
        exponent = sb("exponent", [P, GT, TOP], I32)
        cand = sb("cand", [P, GT, LEVELS * TOP], F32)
        cand_rest = sb("cand_rest", [P, LEVELS * TOP], F32)
        fields = sb("fields", [P, GT, TOP + 2], F32)
        present = sb("present", [P, GT, TOP], F32)
        crowded = sb("crowded", [P, GT], F32)
        usable = sb("usable", [P, GT], F32)
        over6 = sb("over6", [P, GT], F32)
        slow = sb("slow", [P, NT], F32)
        flags = sb("flags", [P, 3, GT], BF16)
        mid_here = sb("mid_here", [P, 1], F32)
        mid_before = sb("mid_before", [P, 1], BF16)
        place = sb("place", [P, 3, GT], F32)
        hot = sb("hot", [P, 2, GT, P], F32)
        hot_mid = sb("hot_mid", [P, GT, MID], F32)
        hotT = sb("hotT", [P, 2, GT * P], F32)
        bl = sb("bl", [P, 2, TOP + 1], F32)
        gone = sb("gone", [P, 2], F32)
        odd = sb("odd", [P, 1], F32)
        kept = sb("kept", [P, TOP], F32)
        keys = sb("keys", [P, SLOTS], F32)
        keys0 = sb("keys0", [P, SLOTS], F32)
        missing = sb("missing", [P, SLOTS], F32)
        idx = sb("idx", [P, SLOTS], U32)
        w_low = sb("w_low", [P, 2, 2], F32)
        ga = sb("ga", [P, SLOTS, D], F32)
        gb = sb("gb", [P, SLOTS, D], F32)
        agg = sb("agg", [P, 2, D], F32)
        combT = sb("combT", [P, CHUNK * P], F32)
        res = sb("res", [P, NC, CHUNK, D], F32)
        mid = sb("mid", [MID, TOP + 2], F32)
        mid_gone = sb("mid_gone", [MID, 3], F32)
        mid_kept = sb("mid_kept", [MID, TOP], F32)
        mid_rest = sb("mid_rest", [MID, TOP], F32)
        mid_top = sb("mid_top", [MID, TOP], F32)
        mid_miss = sb("mid_miss", [MID, TOP], F32)
        mid_row = sb("mid_row", [MID, 1], U32)
        mid_ndiag = sb("mid_ndiag", [MID, MID], F32)
        mid_sel = sb("mid_sel", [P, 4, 8], F32)
        mid_idxf = sb("mid_idxf", [P, 4], F32)
        mid_idx = sb("mid_idx", [P, 4], U32)
        mid_x = sb("mid_x", [MID, D], F32)
        mid_g = sb("mid_g", [P, 4, D], F32)
        mid_s = sb("mid_s", [P, 2, TOP, MID], F32)
        mid_w = sb("mid_w", [P, 4, MID], F32)
        mid_t = sb("mid_t", [P, 2, MID], F32)
        mid_out = sb("mid_out", [MID, D], F32)
        slow_i = sb("slow_i", [P, NT], I32)
        slow_sum = sb("slow_sum", [P, 1], F32)
        slow_n = sb("slow_n", [P, 1], I32)
        slow_row = sb("slow_row", [1, N], I32)
        vals = sb("vals", [P, NP], F32)
        ranked = sb("ranked", [P, NP], F32)
        top8 = sb("top8", [P, 8], F32)
        sc = sb("sc", [P, 24], F32)
        sci = sb("sci", [P, 8], I32)
        x_col = sb("x_col", [P, 1], F32)
        comb_col = sb("comb_col", [P, 1], F32)
        out_col = sb("out_col", [P, 1], F32)
        a_row = adj_ring[0]
        nbr = adj_ring[1][:].bitcast(F32)
        rank = adj_ring[2][:].bitcast(F32)
        xT = mask_ring[:].rearrange("p r n -> p (r n)").bitcast(F32)[:, 0:N]

        ps_words = [psum(f"ps_words{i}", [P, 512]) for i in range(RING)]
        ps_small = psum("ps_small", [P, 512])
        ps_hotT = psum("ps_hotT", [P, 512])
        ps_comb = psum("ps_comb", [P, 512])
        ps_out = psum("ps_out", [P, 512])
        ps_place = ps_small[:, 0:3 * GT].rearrange("p (c t) -> p c t", c=3)
        ps_bl = ps_small[:, 32:32 + 2 * (TOP + 1)].rearrange("p (c f) -> p c f", c=2)
        ps_mid = ps_small[0:MID, 96:96 + TOP + 2]

        s_x = sem("x_loaded")
        s_wb = sem("weights_loaded")
        s_adj = [sem(f"adj_loaded{i}") for i in range(RING)]
        s_pool_step = sem("pool_step")
        s_const = sem("pool_constants_ready")
        s_vconst = sem("vector_constants_ready")
        s_wps = sem("w_transposed")
        s_wT = sem("wT_ready")
        s_raw = sem("adj_as_bf16")
        s_mask = sem("mask_ready")
        s_words = sem("words_packed")
        s_top = sem("words_listed")
        s_flags = sem("flags_ready")
        s_place = sem("places_counted")
        s_hot = sem("hot_ready")
        s_comp = sem("blocks_filled")
        s_idx = sem("indices_ready")
        s_pads = sem("pads_written")
        s_go = sem("gathers_issued")
        s_gath = sem("rows_gathered")
        s_agg = sem("agg_ready")
        s_hps = sem("hotT_in_psum")
        s_hT = sem("hotT_copied")
        s_cps = sem("comb_in_psum")
        s_comb = sem("comb_copied")
        s_ops = sem("out_in_psum")
        s_res = sem("result_ready")
        s_wr = sem("result_written")
        s_step = sem("vector_step")
        s_passed = sem("vector_past_wait")
        s_mpads = sem("mid_pads_written")
        s_mkeys = sem("mid_keys_ready")
        s_mspread = sem("mid_keys_spread")
        s_midx = sem("mid_indices_ready")
        s_mgath = sem("mid_rows_gathered")
        s_mT = sem("mid_transposed")
        s_mS = sem("mid_sorted_layout_ready")
        s_mxT = sem("mid_x_transposed")
        s_mcomb = sem("mid_comb_ready")
        s_mops = sem("mid_out_in_psum")
        s_mres = sem("mid_result_ready")
        s_mwr = sem("mid_written")
        s_slsum = sem("slow_summed")
        s_slps = sem("slow_total_in_psum")
        s_sln = sem("slow_count_ready")
        s_slsc = sem("slow_scratch_written")
        s_slin = sem("slow_inputs_loaded")
        s_ra = sem("slow_row_loaded")
        s_rc = sem("slow_comb_ready")
        s_rp = sem("slow_out_in_psum")
        s_ro = sem("slow_result_ready")
        s_rw = sem("slow_row_written")

        block = ctx.enter_context(nc.Block())

        def groups(eng, front, back):
            front(0, GT, None)
            with eng.Fori(1, NG) as g:
                front(g, GT, back)
            front(NG, TT, back)

        @block.sync
        def _(sp):
            def load(g, i, wait):
                if wait:
                    sp.wait_ge(s_raw, g * GT + (i + 1 - RING))
                t = g * GT + i
                src = adj[LAST:N, :] if isinstance(g, int) and t == NT - 1 else adj[bass.ds(t * P, P), :]
                sp.dma_start(adj_ring[i % RING][:, 0:N], src).then_inc(s_adj[i % RING], 16)

            def front(g, tiles, back):
                for i in range(tiles):
                    load(g, i, wait=back is not None or i >= RING)
                    if back is None and i == 0:
                        sp.dma_start(w_in[:], W).then_inc(s_wb, 16)
                        sp.dma_start(b_row[:], b.rearrange("(a d) -> a d", a=1)).then_inc(s_wb, 16)
                        sp.dma_start(b_col[:], b.rearrange("(d a) -> d a", a=1)).then_inc(s_wb, 16)

            groups(sp, front, True)

            sp.wait_ge(s_sln, 1)
            n_slow = sp.value_load(slow_n[0:1, 0:1], min_val=0, max_val=N)
            with sp.If(n_slow > 0):
                sp.dma_start(flag_rows[0:(NT - 1) * P].rearrange("(t p) -> p t", p=P),
                             slow_i[:, 0:NT - 1], allow_slow_non_contiguous=True).then_inc(s_slsc, 16)
                sp.dma_start(flag_rows[(NT - 1) * P:N].rearrange("(p a) -> p a", a=1),
                             slow_i[NT * P - N:P, NT - 1:NT], allow_slow_non_contiguous=True).then_inc(s_slsc, 16)
                sp.wait_ge(s_mwr, 16)
                sp.wait_ge(s_slsc, 32)
                sp.dma_start(slow_row[:], flag_rows.rearrange("(a n) -> a n", a=1)).then_inc(s_slin, 16)
                sp.dma_start(xT, x.rearrange("n d -> d n"), allow_slow_non_contiguous=True).then_inc(s_slin, 16)
                sp.wait_ge(s_slin, 32)
                with sp.Fori(0, N) as r:
                    is_slow = sp.value_load(slow_row[0:1, bass.ds(r, 1)], min_val=0, max_val=1)
                    with sp.If(is_slow > 0):
                        sp.dma_start(a_row[:, 0:N], adj[bass.ds(r, 1), :].broadcast_to([P, N])).then_inc(s_ra, 16)
                        sp.wait_ge(s_ro, 1)
                        sp.sem_clear(s_ro)
                        sp.dma_start(out[bass.ds(r, 1), :].rearrange("a d -> d a"), out_col[:],
                                     allow_slow_non_contiguous=True).then_inc(s_rw, 16)
                        sp.wait_ge(s_rw, 16)
                        sp.sem_clear(s_rw)

        @block.gpsimd
        def _(pool):
            steps = [0]

            def step(ins):
                steps[0] += 1
                ins.then_inc(s_pool_step, 1)
                pool.wait_ge(s_pool_step, steps[0])

            step(nc.gpsimd.memset(ident[:], 0.0))
            step(nc.gpsimd.affine_select(out=ident[:], in_=ident[:], compare_op=ALU.not_equal, fill=1.0, base=0,
                                         pattern=[[-1, P]], channel_multiplier=1))
            step(nc.gpsimd.memset(ones_bf[:], 1.0))
            step(nc.gpsimd.affine_select(out=before[:], in_=ones_bf[:], compare_op=ALU.is_gt, fill=0.0, base=0,
                                         pattern=[[1, P]], channel_multiplier=-1))
            step(nc.gpsimd.iota(word_no[:], [[1, NW]], base=0, channel_multiplier=0,
                                allow_small_or_imprecise_dtypes=True))
            nc.gpsimd.memset(ones_f[:], 1.0).then_inc(s_const, 1)
            step(nc.gpsimd.iota(dest_no[:], [[1, P]], base=1, channel_multiplier=0,
                                allow_small_or_imprecise_dtypes=True))
            step(nc.gpsimd.iota(slot_no[:], [[1, TOP]], base=0, channel_multiplier=0,
                                allow_small_or_imprecise_dtypes=True))
            step(nc.gpsimd.iota(row_code[:], [[P, NT]], base=-NOROW, channel_multiplier=1,
                                allow_small_or_imprecise_dtypes=True))
            step(nc.gpsimd.iota(row_code[:, NT - 1:NT], [[0, 1]], base=LAST - NOROW, channel_multiplier=1,
                                allow_small_or_imprecise_dtypes=True))
            step(nc.gpsimd.memset(counts_here[:], 1.0))
            step(nc.gpsimd.memset(counts_here[0:NT * P - N, NT - 1:NT], 0.0))
            step(nc.gpsimd.memset(pads[:, 0, :], -BIG))
            step(nc.gpsimd.memset(pads[:, 1, :], BIG))
            step(nc.gpsimd.memset(ga[:], 0.0))
            step(nc.gpsimd.memset(gb[:], 0.0))
            step(nc.gpsimd.memset(mid_x[:], 0.0))
            step(nc.gpsimd.iota(spread[:], [[16, 2], [1, 16], [0, 8]], base=0, channel_multiplier=-1,
                                allow_small_or_imprecise_dtypes=True))
            step(nc.gpsimd.iota(part_i[:], [[0, 1]], base=0, channel_multiplier=1))
            nc.gpsimd.iota(col_no[:], [[1, NP]], base=0, channel_multiplier=0,
                           allow_small_or_imprecise_dtypes=True).then_inc(s_const, 1)

            def load_x(g, tiles):
                if tiles == GT:
                    pool.dma_start(x_grp[:], x[bass.ds(g * (GT * P), GT * P), :].rearrange("(t p) d -> p t d", p=P)
                                   ).then_inc(s_x, 16)
                else:
                    pool.dma_start(x_grp[:, 0:TT - 1, :],
                                   x[NG * GT * P:(NT - 1) * P, :].rearrange("(t p) d -> p t d", p=P)).then_inc(s_x, 16)
                    pool.dma_start(x_grp[:, TT - 1, :], x[LAST:N, :]).then_inc(s_x, 16)

            def back(g, tiles):
                for c in range(-(-tiles // CHUNK)):
                    pool.wait_ge(s_res, g * NC + (c + 1))
                    pool.sem_inc(s_go, 1)
                    n = min(CHUNK, tiles - c * CHUNK)
                    if tiles == GT:
                        rows = out[bass.ds(g * (GT * P) + c * CHUNK * P, n * P), :]
                        pool.dma_start(rows.rearrange("(t p) d -> p t d", p=P), res[:, c, 0:n, :]).then_inc(s_wr, 16)
                    else:
                        first = (NG * GT) * P
                        pool.dma_start(out[first:LAST + 1, :].rearrange("(t p) d -> p t d", p=P),
                                       res[:, 0, 0:TT - 1, :]).then_inc(s_wr, 16)
                        pool.dma_start(out[LAST + 1:LAST + 113, :], res[1:113, 0, TT - 1, :]).then_inc(s_wr, 16)
                        pool.dma_start(out[LAST + 113:N, :], res[113:P, 0, TT - 1, :]).then_inc(s_wr, 16)

            def front(g, tiles, bk):
                if bk and tiles == GT:
                    back(g - 1, GT)
                    load_x(g, GT)
                pool.wait_ge(s_idx, g + 1)
                pool.wait_ge(s_pads, g + 1)
                pool.sem_inc(s_go, 1)
                for s in range(SLOTS):
                    nc.gpsimd.indirect_dma_start(
                        ga[:, s, :], None, x, bass.IndirectOffsetOnAxis(ap=idx[:, s:s + 1], axis=0),
                        bounds_check=N - 1, oob_is_err=False).then_inc(s_gath, 16)

            load_x(0, GT)
            groups(pool, front, True)
            pool.wait_ge(s_midx, 1)
            nc.gpsimd.indirect_dma_start(mid_x[:], None, x, bass.IndirectOffsetOnAxis(ap=mid_row[:], axis=0),
                                         bounds_check=N - 1, oob_is_err=False).then_inc(s_mgath, 16)
            pool.wait_ge(s_midx, 2)
            pool.wait_ge(s_mpads, 1)
            for u in range(4):
                nc.gpsimd.indirect_dma_start(mid_g[:, u, :], None, x,
                                             bass.IndirectOffsetOnAxis(ap=mid_idx[:, u:u + 1], axis=0),
                                             bounds_check=N - 1, oob_is_err=False).then_inc(s_mgath, 16)
            back(NG - 1, GT)
            load_x(NG, TT)
            back(NG, TT)
            pool.wait_ge(s_mres, 1)
            pool.wait_ge(s_wr, 16 * (NG * NC + 3))
            nc.gpsimd.indirect_dma_start(out, bass.IndirectOffsetOnAxis(ap=mid_row[:], axis=0), mid_out[:], None,
                                         bounds_check=N - 1, oob_is_err=False).then_inc(s_mwr, 16)
            pool.wait_ge(s_mwr, 16)

        @block.scalar
        def _(act):
            def to_bf16(g, i, wait):
                act.wait_ge(s_adj[i % RING], g * (GT // RING * 16) + 16 * (i // RING + 1))
                if wait:
                    act.wait_ge(s_words, g * GT + (i + 1 - RING))
                else:
                    act.wait_ge(s_vconst, 1)
                nc.scalar.activation(mask_ring[:, i % RING, :], adj_ring[i % RING][:], ACT.Copy).then_inc(s_raw, 1)

            def hot_copies(g, tiles):
                for c in range(-(-tiles // CHUNK)):
                    n = min(CHUNK, tiles - c * CHUNK) * P
                    for k in range(2):
                        act.wait_ge(s_hps, g * (2 * NC) + (2 * c + k + 1))
                        if not isinstance(g, int) or g >= 1:
                            act.wait_ge(s_cps, g * NC)
                        nc.scalar.activation(hotT[:, k, c * CHUNK * P:c * CHUNK * P + n], ps_hotT[:, 0:n],
                                             ACT.Copy).then_inc(s_hT, 1)

            def comb_copies(g, tiles):
                for c in range(-(-tiles // CHUNK)):
                    n = min(CHUNK, tiles - c * CHUNK) * P
                    act.wait_ge(s_cps, g * NC + (c + 1))
                    if not (isinstance(g, int) and g == 0 and c == 0):
                        act.wait_ge(s_ops, g * NC + c)
                    nc.scalar.activation(combT[:, 0:n], ps_comb[:, 0:n], ACT.Copy).then_inc(s_comb, 1)

            def write_pads(g):
                if not (isinstance(g, int) and g == 0):
                    act.wait_ge(s_agg, g)
                else:
                    act.wait_ge(s_const, 2)
                nc.scalar.activation(ga[:, SLOTS - 2:SLOTS, :], pads[:], ACT.Copy).then_inc(s_pads, 1)

            def front(g, tiles, back):
                for i in range(tiles):
                    to_bf16(g, i, wait=back is not None or i >= RING)
                    if back is None and i == 0:
                        act.wait_ge(s_wps, 1)
                        nc.scalar.activation(wT[:], ps_comb[:, 0:D], ACT.Copy).then_inc(s_wT, 1)
                    if back and i == min(2, tiles - 1):
                        hot_copies(g - 1, GT)
                if back:
                    write_pads(g)
                    comb_copies(g - 1, GT)
                else:
                    write_pads(g)

            groups(act, front, True)
            for u in range(4):
                last = nc.scalar.activation(mid_g[:, u, :], mid_pads[:], ACT.Copy)
            last.then_inc(s_mpads, 1)
            hot_copies(NG, TT)
            comb_copies(NG, TT)
            act.wait_ge(s_mT, 1)
            for u in range(4):
                h, sh = u // 2, u % 2
                last = nc.scalar.activation(mid_s[:, 0, sh * 8:sh * 8 + 8, h * 16:h * 16 + 16],
                                            ps_hotT[:, u * P:(u + 1) * P].rearrange("p (b s) -> p s b", s=8), ACT.Copy)
            last.then_inc(s_mS, 1)

        @block.tensor
        def _(pe):
            pe.wait_ge(s_const, 1)
            pe.wait_ge(s_wb, 48)
            nc.tensor.transpose(ps_comb[:, 0:D], w_in[:], ident[:]).then_inc(s_wps, 1)
            pe.wait_ge(s_vconst, 1)

            def pack(g, i, wait):
                pe.wait_ge(s_mask, g * GT + (i + 1))
                if wait:
                    pe.wait_ge(s_top, g * GT + (i + 1 - RING))
                bank = ps_words[i % RING][:, 0:NW]
                nc.tensor.matmul(bank, ones_bf[0:1, :], word_no[0:1, :], start=True, stop=False)
                for k in range(BITS):
                    last = nc.tensor.matmul(bank, bit_diag[:, k, :], mask_ring[:, i % RING, k * NW:(k + 1) * NW],
                                            start=False, stop=(k == BITS - 1))
                last.then_inc(s_words, 1)

            def turn_hot(g, tiles):
                for c in range(-(-tiles // CHUNK)):
                    for k in range(2):
                        n = min(CHUNK, tiles - c * CHUNK)
                        pe.wait_ge(s_hot, g + 1)
                        if not (isinstance(g, int) and g == 0 and c == 0 and k == 0):
                            pe.wait_ge(s_hT, g * (2 * NC) + (2 * c + k))
                        for i in range(n):
                            last = nc.tensor.transpose(ps_hotT[:, i * P:(i + 1) * P], hot[:, k, c * CHUNK + i, :],
                                                       ident[:])
                        last.then_inc(s_hps, 1)

            def combine(g, tiles, c, n):
                pe.wait_ge(s_agg, g + 1)
                pe.wait_ge(s_hT, g * (2 * NC) + (2 * c + 2))
                pe.wait_ge(s_x, g * 16 + (16 if tiles == GT else 32))
                if isinstance(g, int) and g == 0 and c == 0:
                    pe.wait_ge(s_wT, 1)
                else:
                    pe.wait_ge(s_comb, g * NC + c)
                for k in range(2):
                    nc.tensor.matmul(ps_comb[:, 0:n * P], agg[:, k, :], hotT[:, k, c * CHUNK * P:(c * CHUNK + n) * P],
                                     start=(k == 0), stop=False)
                for i in range(n):
                    last = nc.tensor.matmul(ps_comb[:, i * P:(i + 1) * P], x_grp[:, c * CHUNK + i, :],
                                            half_ident[:], start=False, stop=(i == n - 1))
                last.then_inc(s_cps, 1)

            def project(g, c, n):
                pe.wait_ge(s_comb, g * NC + (c + 1))
                if not (isinstance(g, int) and g == 0 and c == 0):
                    pe.wait_ge(s_res, g * NC + c)
                for i in range(n):
                    nc.tensor.matmul(ps_out[:, i * P:(i + 1) * P], combT[:, i * P:(i + 1) * P], wT[:],
                                     start=True, stop=False)
                    last = nc.tensor.matmul(ps_out[:, i * P:(i + 1) * P], ones_f[0:1, :], b_row[:],
                                            start=False, stop=True)
                last.then_inc(s_ops, 1)

            def dense(g, tiles):
                for c in range(-(-tiles // CHUNK)):
                    if c:
                        project(g, c - 1, CHUNK)
                    combine(g, tiles, c, min(CHUNK, tiles - c * CHUNK))

            def dense_end(g, tiles):
                c = -(-tiles // CHUNK) - 1
                project(g, c, tiles - c * CHUNK)

            def places(g, tiles):
                pe.wait_ge(s_flags, g + 1)
                nc.tensor.matmul(ps_place[:, :, 0:tiles], before[:], flags[:, :, 0:tiles], start=True, stop=False)
                for d in range(1, tiles):
                    nc.tensor.matmul(ps_place[:, :, d:tiles], ones_bf[:], flags[:, :, 0:tiles - d],
                                     start=False, stop=False)
                for i in range(tiles):
                    last = nc.tensor.matmul(ps_place[:, 2, i:i + 1], ones_bf[:], mid_before[:], start=False,
                                            stop=(i == tiles - 1))
                last.then_inc(s_place, 1)

            def fill_blocks(g, tiles):
                pe.wait_ge(s_hot, g + 1)
                for k in range(2):
                    for i in range(tiles):
                        nc.tensor.matmul(ps_bl[:, k, :], hot[:, k, i, :], fields[:, i, 0:TOP + 1],
                                         start=(i == 0), stop=(i == tiles - 1))
                for i in range(tiles):
                    last = nc.tensor.matmul(ps_mid, hot_mid[:, i, :], fields[:, i, :], start=(i == 0),
                                            stop=(i == tiles - 1))
                last.then_inc(s_comp, 1)

            def front(g, tiles, back):
                for i in range(tiles):
                    if back and tiles == GT and i == tiles - 1:
                        dense(g - 1, GT)
                    pack(g, i, wait=back is not None or i >= RING)
                    if back and i == 1:
                        turn_hot(g - 1, GT)
                if back and tiles == GT:
                    dense_end(g - 1, GT)
                if back and tiles < GT:
                    dense(g - 1, GT)
                places(g, tiles)
                fill_blocks(g, tiles)
                if back and tiles < GT:
                    dense_end(g - 1, GT)

            groups(pe, front, True)
            turn_hot(NG, TT)
            pe.wait_ge(s_mkeys, 1)
            for h in range(2):
                nc.tensor.matmul(ps_words[0][:, h * TOP:(h + 1) * TOP], spread[:, h, :], mid_top[:],
                                 start=True, stop=True)
            nc.tensor.matmul(ps_words[0][:, 64:64 + MID], ones_f[0:MID, :], mid_ndiag[:], start=True,
                             stop=True).then_inc(s_mspread, 1)
            dense(NG, TT)
            dense_end(NG, TT)
            pe.wait_ge(s_mgath, 16 * 5)
            pe.wait_ge(s_hT, 2 * NC * NG + 2)
            for u in range(4):
                last = nc.tensor.transpose(ps_hotT[:, u * P:(u + 1) * P], mid_g[:, u, :], ident[:])
            last.then_inc(s_mT, 1)
            nc.tensor.matmul(ps_words[1][:, 0:MID], mid_x[:], half_ident[0:MID, 0:MID], start=True,
                             stop=True).then_inc(s_mxT, 1)
            pe.wait_ge(s_mcomb, 1)
            nc.tensor.matmul(ps_words[2][0:MID, 0:D], mid_t[:, 1, :], wT[:], start=True, stop=False)
            nc.tensor.matmul(ps_words[2][0:MID, 0:D], ones_f[0:1, 0:MID], b_row[:], start=False,
                             stop=True).then_inc(s_mops, 1)
            pe.wait_ge(s_slsum, 1)
            nc.tensor.matmul(ps_small[:, 0:1], ones_f[:], slow_sum[:], start=True, stop=True).then_inc(s_slps, 1)
            pe.wait_ge(s_sln, 1)
            n_slow = pe.value_load(slow_n[0:1, 0:1], min_val=0, max_val=N)
            with pe.If(n_slow > 0):
                pe.wait_ge(s_slin, 32)
                with pe.Fori(0, N) as r:
                    is_slow = pe.value_load(slow_row[0:1, bass.ds(r, 1)], min_val=0, max_val=1)
                    with pe.If(is_slow > 0):
                        pe.wait_ge(s_rc, 1)
                        pe.sem_clear(s_rc)
                        nc.tensor.matmul(ps_out[:, 0:1], wT[:], comb_col[:], start=True, stop=True).then_inc(s_rp, 1)

        @block.vector
        def _(dve):
            v = nc.vector
            steps = [0]

            def step(ins):
                steps[0] += 1
                ins.then_inc(s_step, 1)
                dve.wait_ge(s_step, steps[0])

            def restart():
                dve.sem_clear(s_step)
                steps[0] = 0

            for i in range(RING):
                step(v.memset(adj_ring[i][:, N:NP], 0))
            step(v.memset(mid[:], 0.0))
            step(v.memset(mid_before[:], 0.0))
            step(v.memset(slow[:], 0.0))
            dve.wait_ge(s_const, 1)
            step(v.tensor_copy(ident_bf[:], ident[:]))
            step(v.tensor_scalar(half_ident[:], ident[:], 0.5, None, ALU.mult))
            for k in range(BITS):
                last = v.tensor_scalar(bit_diag[:, k, :], ident_bf[:], float(2 ** (k + 8)), None, ALU.mult)
            last.then_inc(s_vconst, 1)
            dve.wait_ge(s_const, 2)
            step(v.tensor_scalar(spread[:], spread[:], 0.0, None, ALU.is_equal))
            step(v.tensor_scalar(part_a[:], part_i[:], 7, None, ALU.bitwise_and))
            step(v.tensor_copy(part_f[:, 0:1], part_a[:]))
            step(v.tensor_scalar(part_a[:], part_i[:], 1, None, ALU.bitwise_and))
            step(v.tensor_copy(part_f[:, 1:2], part_a[:]))
            step(v.tensor_scalar(own_slot[:], slot_no[:, 0:8], part_f[:, 0:1], None, ALU.is_equal))
            step(v.tensor_scalar(sign_f[:], part_f[:, 1:2], 2.0, -1.0, ALU.mult, ALU.add))
            step(v.tensor_scalar(mid_pads[:], pads[:, 1, :], sign_f[:, 0:1], None, ALU.mult))

            def make_mask(g, i):
                dve.wait_ge(s_raw, g * GT + (i + 1))
                m = mask_ring[:, i % RING, :]
                v.tensor_scalar(m, m, 0.0, None, ALU.not_equal).then_inc(s_mask, 1)

            def list_words(g, i):
                dve.wait_ge(s_words, g * GT + (i + 1))
                dve.sem_inc(s_passed, 1)
                bank = ps_words[i % RING][:, 0:NW]
                step(v.max(words[:, i, 0:8], bank))
                step(v.match_replace(rest_words[:], words[:, i, 0:8], bank, -1.0))
                v.max(words[:, i, 8:16], rest_words[:]).then_inc(s_top, 1)

            def decode(g, tiles):
                w, wi = words[:, 0:tiles, :], words_i[:, 0:tiles, :]
                lo, base = low_i[:, 0:tiles, :], col_base[:, 0:tiles, :]
                rs, hb, ex = rest[:, 0:tiles, :], high_bit[:, 0:tiles, :], exponent[:, 0:tiles, :]
                dve.wait_ge(s_top, g * GT + tiles)
                step(v.tensor_copy(wi, w))
                step(v.tensor_scalar(lo, wi, 255, None, ALU.bitwise_and))
                step(v.tensor_scalar(base, lo, float(1 - NW * (127 + 8)), None, ALU.add))
                step(v.tensor_tensor(rs, w, lo, ALU.subtract))
                for l in range(LEVELS):
                    step(v.tensor_scalar(hb.bitcast(I32), rs.bitcast(I32), EXPONENT, None, ALU.bitwise_and))
                    step(v.tensor_scalar(ex, rs.bitcast(I32), 23, None, ALU.logical_shift_right))
                    step(v.scalar_tensor_tensor(out=cand[:, 0:tiles, l * TOP:(l + 1) * TOP], in0=ex, scalar=float(NW),
                                                in1=base, op0=ALU.mult, op1=ALU.add))
                    step(v.tensor_tensor(rs, rs, hb, ALU.subtract))
                step(v.tensor_reduce(crowded[:, 0:tiles], rs, AX.X, ALU.max))
                for i in range(tiles):
                    step(v.max(fields[:, i, 0:8], cand[:, i, :]))
                    step(v.match_replace(cand_rest[:], fields[:, i, 0:8], cand[:, i, :], -1e6))
                    step(v.max(fields[:, i, 8:16], cand_rest[:]))
                nb = fields[:, 0:tiles, 0:TOP]
                count = fields[:, 0:tiles, TOP]
                step(v.tensor_copy(fields[:, 0:tiles, TOP + 1], row_code[:, bass.ds(g * GT, tiles)]))
                step(v.tensor_scalar(present[:, 0:tiles, :], nb, 0.0, None, ALU.is_gt))
                step(v.tensor_reduce(count, present[:, 0:tiles, :], AX.X, ALU.add))
                cr, ok, o6 = crowded[:, 0:tiles], usable[:, 0:tiles], over6[:, 0:tiles]
                here = counts_here[:, bass.ds(g * GT, tiles)]
                step(v.scalar_tensor_tensor(out=cr, in0=words[:, 0:tiles, TOP - 1], scalar=256.0, in1=cr,
                                            op0=ALU.is_ge, op1=ALU.max))
                step(v.scalar_tensor_tensor(out=cr, in0=fields[:, 0:tiles, TOP - 1], scalar=0.0, in1=cr,
                                            op0=ALU.is_gt, op1=ALU.max))
                step(v.scalar_tensor_tensor(out=ok, in0=cr, scalar=0.0, in1=here, op0=ALU.is_equal, op1=ALU.mult))
                step(v.scalar_tensor_tensor(out=slow[:, bass.ds(g * GT, tiles)], in0=cr, scalar=0.0, in1=here,
                                            op0=ALU.is_gt, op1=ALU.mult))
                step(v.scalar_tensor_tensor(out=flags[:, 0, 0:tiles], in0=count, scalar=6.0, in1=ok,
                                            op0=ALU.is_equal, op1=ALU.mult))
                step(v.scalar_tensor_tensor(out=o6, in0=count, scalar=7.0, in1=ok, op0=ALU.is_ge, op1=ALU.mult))
                step(v.scalar_tensor_tensor(out=flags[:, 1, 0:tiles], in0=count, scalar=10.0, in1=o6,
                                            op0=ALU.is_le, op1=ALU.mult))
                v.scalar_tensor_tensor(out=flags[:, 2, 0:tiles], in0=count, scalar=11.0, in1=ok,
                                       op0=ALU.is_ge, op1=ALU.mult).then_inc(s_flags, 1)

            def assign(g, tiles):
                dve.wait_ge(s_place, g + 1)
                pl = place[:, :, 0:tiles]
                step(v.scalar_tensor_tensor(out=pl, in0=ps_place[:, :, 0:tiles], scalar=1.0,
                                            in1=flags[:, :, 0:tiles], op0=ALU.add, op1=ALU.mult))
                step(v.tensor_reduce(mid_here[:], flags[:, 2, 0:tiles], AX.X, ALU.add))
                step(v.tensor_tensor(mid_before[:], mid_before[:], mid_here[:], ALU.add))
                sl = slow[:, bass.ds(g * GT, tiles)]
                for k, room in ((0, P), (1, P), (2, MID)):
                    step(v.scalar_tensor_tensor(out=sl, in0=place[:, k, 0:tiles], scalar=float(room), in1=sl,
                                                op0=ALU.is_gt, op1=ALU.max))
                if not isinstance(g, int) or g > 0:
                    dve.wait_ge(s_hps, g * (2 * NC))
                for k in range(2):
                    for i in range(tiles):
                        v.tensor_scalar(hot[:, k, i, :], dest_no[:], place[:, k, i:i + 1], None, ALU.is_equal)
                for i in range(tiles):
                    last = v.tensor_scalar(hot_mid[:, i, :], dest_no[:, 0:MID], place[:, 2, i:i + 1], None,
                                           ALU.is_equal)
                last.then_inc(s_hot, 1)

            def block_indices(g, par):
                dve.wait_ge(s_comp, g + 1)
                step(v.tensor_copy(bl[:], ps_bl))
                step(v.tensor_tensor(mid[:], mid[:], ps_mid, ALU.add))
                step(v.tensor_copy(keys[:, 0:4].rearrange("p (a c) -> p a c", a=2),
                                   bl[:, 0, 1:7].rearrange("p (a c) -> p a c", a=2)[:, :, 0:2]))
                n = bl[:, 1, TOP:TOP + 1]
                step(v.tensor_scalar(gone[:, 0:1], n, 8.0, 3.0, ALU.is_ge, ALU.add))
                step(v.scalar_tensor_tensor(out=gone[:, 1:2], in0=n, scalar=10.0, in1=gone[:, 0:1], op0=ALU.is_ge,
                                            op1=ALU.add))
                step(v.scalar_tensor_tensor(out=odd[:], in0=gone[:, 1:2], scalar=-2.0, in1=n, op0=ALU.mult,
                                            op1=ALU.add))
                step(v.scalar_tensor_tensor(out=kept[:], in0=slot_no[:], scalar=gone[:, 1:2], in1=bl[:, 1, 0:TOP],
                                            op0=ALU.not_equal, op1=ALU.mult))
                step(v.tensor_scalar(kept[:, 0:1], kept[:, 0:1], odd[:, 0:1], None, ALU.mult))
                step(v.max(keys[:, 4:12], kept[:]))
                step(v.tensor_scalar(w_low[:, par, 0:1], n, 9.0, THIRD_HALF, ALU.is_ge, ALU.mult))
                step(v.tensor_scalar(w_low[:, par, 1:2], n, 9.0, THIRD_HALF, ALU.is_lt, ALU.mult))
                step(v.tensor_scalar(keys0[:], keys[:], 0.0, -1.0, ALU.max, ALU.add))
                step(v.tensor_scalar(missing[:], keys[:], 0.0, float(NOROW + 1), ALU.is_le, ALU.mult))
                if not isinstance(g, int) or g > 0:
                    dve.wait_ge(s_gath, g * (SLOTS * 16))
                v.tensor_tensor(idx[:], keys0[:], missing[:], ALU.add).then_inc(s_idx, 1)

            def low_high(dst_lo, dst_hi, a, c):
                if dst_lo is not None:
                    v.tensor_tensor(dst_lo, a, c, ALU.min).then_inc(s_step, 1)
                    steps[0] += 1
                if dst_hi is not None:
                    v.tensor_tensor(dst_hi, a, c, ALU.max).then_inc(s_step, 1)
                    steps[0] += 1

            def layer_done():
                dve.wait_ge(s_step, steps[0])

            def sort_and_pool(g, par):
                dve.wait_ge(s_gath, g * (SLOTS * 16) + SLOTS * 16)
                pa = ga[:].rearrange("p (a c) d -> p a c d", c=2)
                pb = gb[:].rearrange("p (a c) d -> p a c d", c=2)
                low_high(pb[:, :, 0, :], pb[:, :, 1, :], pa[:, :, 0, :], pa[:, :, 1, :])
                layer_done()
                qa = ga[:].rearrange("p (q h c) d -> p q h (c d)", q=3, h=2)
                qb = gb[:].rearrange("p (q h c) d -> p q h (c d)", q=3, h=2)
                low_high(qa[:, :, 0, :], qa[:, :, 1, :], qb[:, :, 0, :], qb[:, :, 1, :])
                layer_done()
                la = ga[:].rearrange("p (q l) d -> p q l d", q=3)
                lb = gb[:].rearrange("p (q l) d -> p q l d", q=3)
                low_high(lb[:, :, 1, :], lb[:, :, 2, :], la[:, :, 1, :], la[:, :, 2, :])
                layer_done()
                A, B = ga[:, 4:12, :], gb[:, 4:12, :]
                low_high(None, B[:, 4, :], A[:, 0, :], A[:, 4, :])
                low_high(B[:, 3, :], None, A[:, 3, :], A[:, 7, :])
                low_high(A[:, 1:3, :], A[:, 5:7, :], B[:, 1:3, :], B[:, 5:7, :])
                layer_done()
                low_high(B[:, 2, :], A[:, 4, :], A[:, 2, :], B[:, 4, :])
                low_high(A[:, 3, :], B[:, 5, :], B[:, 3, :], A[:, 5, :])
                layer_done()
                low_high(B[:, 1, :], A[:, 2, :], A[:, 1, :], B[:, 2, :])
                low_high(B[:, 3, :], None, A[:, 3, :], A[:, 4, :])
                low_high(A[:, 5, :], None, B[:, 5, :], A[:, 6, :])
                layer_done()
                if not isinstance(g, int) or g > 0:
                    dve.wait_ge(s_cps, g * NC)
                a0, a1 = agg[:, 0, :], agg[:, 1, :]
                w = THIRD_HALF
                step(v.tensor_scalar(a0, ga[:, 0, :], w, None, ALU.mult))
                step(v.tensor_scalar(a1, B[:, 1, :], w_low[:, par, 0:1], None, ALU.mult))
                step(v.scalar_tensor_tensor(out=a0, in0=gb[:, 1, :], scalar=w, in1=a0, op0=ALU.mult, op1=ALU.add))
                step(v.scalar_tensor_tensor(out=a1, in0=A[:, 2, :], scalar=w_low[:, par, 1:2], in1=a1,
                                            op0=ALU.mult, op1=ALU.add))
                step(v.scalar_tensor_tensor(out=a0, in0=gb[:, 2, :], scalar=w, in1=a0, op0=ALU.mult, op1=ALU.add))
                step(v.scalar_tensor_tensor(out=a1, in0=B[:, 3, :], scalar=w, in1=a1, op0=ALU.mult, op1=ALU.add))
                v.scalar_tensor_tensor(out=a1, in0=A[:, 5, :], scalar=w, in1=a1, op0=ALU.mult,
                                       op1=ALU.add).then_inc(s_agg, 1)

            def add_self(g, tiles):
                for c in range(-(-tiles // CHUNK)):
                    n = min(CHUNK, tiles - c * CHUNK)
                    dve.wait_ge(s_x, g * 16 + (16 if tiles == GT else 32))
                    dve.wait_ge(s_ops, g * NC + (c + 1))
                    if not isinstance(g, int) or g > 0:
                        dve.wait_ge(s_wr, g * (NC * 16))
                    v.tensor_tensor(res[:, c, 0:n, :], ps_out[:, 0:n * P].rearrange("p (t d) -> p t d", d=D),
                                    x_grp[:, c * CHUNK:c * CHUNK + n, :], ALU.add).then_inc(s_res, 1)

            def front(g, tiles, back):
                restart()
                make_mask(g, 0)
                for i in range(1, tiles):
                    if back and tiles == GT and i == tiles - 1:
                        sort_and_pool(g - 1, 0)
                    make_mask(g, i)
                    list_words(g, i - 1)
                list_words(g, tiles - 1)
                if back and tiles < GT:
                    sort_and_pool(g - 1, 0)
                if back and tiles == GT:
                    add_self(g - 1, GT)
                decode(g, tiles)
                assign(g, tiles)
                block_indices(g, 0)

            groups(dve, front, True)

            add_self(NG - 1, GT)
            n = mid[:, TOP:TOP + 1]
            step(v.tensor_scalar(mid_row[:], mid[:, TOP + 1:TOP + 2], float(NOROW), None, ALU.add))
            step(v.tensor_scalar(mid_gone[:, 0:1], n, 12.0, 5.0, ALU.is_ge, ALU.add))
            step(v.scalar_tensor_tensor(out=mid_gone[:, 1:2], in0=n, scalar=14.0, in1=mid_gone[:, 0:1], op0=ALU.is_ge,
                                        op1=ALU.add))
            step(v.scalar_tensor_tensor(out=mid_gone[:, 2:3], in0=mid_gone[:, 1:2], scalar=-2.0, in1=n, op0=ALU.mult,
                                        op1=ALU.add))
            step(v.scalar_tensor_tensor(out=mid_kept[:], in0=slot_no[0:MID, :], scalar=mid_gone[:, 1:2],
                                        in1=mid[:, 0:TOP], op0=ALU.not_equal, op1=ALU.mult))
            step(v.tensor_scalar(mid_kept[:, 0:1], mid_kept[:, 0:1], mid_gone[:, 2:3], None, ALU.mult))
            step(v.max(mid_top[:, 0:8], mid_kept[:]))
            step(v.match_replace(mid_rest[:], mid_top[:, 0:8], mid_kept[:], -1e6))
            step(v.max(mid_top[:, 8:16], mid_rest[:]))
            step(v.tensor_scalar(mid_miss[:], mid_top[:], 0.0, float(NOROW + 1), ALU.is_le, ALU.mult))
            step(v.tensor_scalar(mid_top[:], mid_top[:], 0.0, -1.0, ALU.max, ALU.add))
            step(v.tensor_tensor(mid_top[:], mid_top[:], mid_miss[:], ALU.add))
            step(v.tensor_scalar(mid_ndiag[:], ident[0:MID, 0:MID], mid[:, TOP:TOP + 1], None, ALU.mult))
            v.tensor_reduce(slow_sum[:], slow[:], AX.X, ALU.add).then_inc(s_slsum, 1)
            v.tensor_scalar(slow_i[:], slow[:], 0.0, None, ALU.add).then_inc(s_mkeys, 1)
            dve.wait_ge(s_mkeys, 1)
            dve.sem_inc(s_midx, 1)
            dve.wait_ge(s_mspread, 1)
            spread_keys = ps_words[0][:, 0:2 * TOP].rearrange("p (u c) -> p u c", c=8)
            for u in range(4):
                last = v.tensor_tensor(mid_sel[:, u, :], spread_keys[:, u, :], own_slot[:], ALU.mult)
            step(last)
            step(v.tensor_reduce(mid_idxf[:], mid_sel[:], AX.X, ALU.add))
            v.tensor_copy(mid_idx[:], mid_idxf[:]).then_inc(s_midx, 1)
            n_all = ps_words[0][:, 64:64 + MID]
            for q, (edge, op) in enumerate(((13.0, ALU.is_ge), (13.0, ALU.is_lt), (15.0, ALU.is_lt), (15.0, ALU.is_ge))):
                step(v.tensor_scalar(mid_w[:, q, :], n_all, edge, THIRD_HALF, op, ALU.mult))

            sort_and_pool(NG, 0)

            dve.wait_ge(s_mS, 1)
            home = [0]

            def lines(buf, start, groups_, gstep, run):
                a = mid_s[:, buf, :, :]
                if groups_ == 1:
                    return a[:, start:start + run, :]
                if run == 1:
                    return a[:, start:start + (groups_ - 1) * gstep + 1:gstep, :]
                end = start + groups_ * gstep
                if end <= TOP:
                    return a[:, start:end, :].rearrange("p (g r) m -> p g r m", g=groups_)[:, :, 0:run, :]
                lead = gstep - run
                return a[:, start - lead:start + (groups_ - 1) * gstep + run, :].rearrange(
                    "p (g r) m -> p g r m", g=groups_)[:, :, lead:gstep, :]

            def layer(pairs, copies):
                src, dst = home[0], 1 - home[0]
                for lo, hi, g_, st, run in pairs:
                    low_high(lines(dst, lo, g_, st, run), lines(dst, hi, g_, st, run),
                             lines(src, lo, g_, st, run), lines(src, hi, g_, st, run))
                for at, g_, st, run in copies:
                    v.tensor_copy(lines(dst, at, g_, st, run), lines(src, at, g_, st, run)).then_inc(s_step, 1)
                    steps[0] += 1
                layer_done()
                home[0] = dst

            layer([(0, 1, 8, 2, 1)], [])
            layer([(0, 2, 4, 4, 2)], [])
            layer([(1, 2, 4, 4, 1)], [(0, 4, 4, 1), (3, 4, 4, 1)])
            layer([(0, 4, 2, 8, 4)], [])
            layer([(2, 4, 1, 8, 2), (10, 12, 1, 8, 2)], [(0, 1, 1, 2), (6, 1, 1, 4), (14, 1, 1, 2)])
            layer([(1, 2, 3, 2, 1), (9, 10, 3, 2, 1)], [(0, 1, 1, 1), (7, 1, 1, 2), (15, 1, 1, 1)])
            layer([(0, 8, 1, 8, 8)], [])
            layer([(4, 8, 1, 4, 4)], [(2, 1, 1, 2), (12, 1, 1, 2)])
            layer([(2, 4, 3, 4, 2)], [])
            layer([(3, 4, 5, 2, 1)], [])
            rk = mid_s[:, home[0], :, :]
            t0, t1 = mid_t[:, 0, :], mid_t[:, 1, :]
            step(v.tensor_tensor(t1, rk[:, 4, :], mid_w[:, 0, :], ALU.mult))
            step(v.tensor_tensor(t0, rk[:, 5, :], mid_w[:, 1, :], ALU.mult))
            step(v.tensor_tensor(t1, t1, t0, ALU.add))
            step(v.scalar_tensor_tensor(out=t1, in0=rk[:, 7, :], scalar=THIRD_HALF, in1=t1, op0=ALU.mult, op1=ALU.add))
            for r_, q in ((10, 2), (11, 3)):
                step(v.tensor_tensor(t0, rk[:, r_, :], mid_w[:, q, :], ALU.mult))
                step(v.tensor_tensor(t1, t1, t0, ALU.add))
            dve.wait_ge(s_mxT, 1)
            v.tensor_tensor(t1, t1, ps_words[1][:, 0:MID], ALU.add).then_inc(s_mcomb, 1)

            add_self(NG, TT)
            dve.wait_ge(s_mops, 1)
            v.tensor_tensor(mid_out[:], ps_words[2][0:MID, 0:D], mid_x[:], ALU.add).then_inc(s_mres, 1)
            dve.wait_ge(s_slps, 1)
            v.tensor_copy(slow_n[:], ps_small[:, 0:1]).then_inc(s_sln, 1)

            dve.wait_ge(s_sln, 1)
            n_slow = dve.value_load(slow_n[0:1, 0:1], min_val=0, max_val=N)
            with dve.If(n_slow > 0):
                restart()
                step(v.memset(ranked[:], 0.0))
                dve.wait_ge(s_slin, 32)
                with dve.Fori(0, N) as r:
                    is_slow = dve.value_load(slow_row[0:1, bass.ds(r, 1)], min_val=0, max_val=1)
                    with dve.If(is_slow > 0):
                        restart()
                        step(v.tensor_copy(x_col[:], xT[:, bass.ds(r, 1)]))
                        dve.wait_ge(s_ra, 16)
                        dve.sem_clear(s_ra)
                        nb, rk_ = nbr[:, 0:N], rank[:, 0:N]
                        step(v.tensor_scalar(nb, a_row[:, 0:N], 0.0, None, ALU.not_equal))
                        step(v.tensor_tensor_scan(rk_, nb, nb, 0.0, ALU.add, ALU.bypass))
                        cnt = rank[:, N - 1:N]
                        step(v.tensor_copy(sci[:, 0:1], cnt))
                        step(v.tensor_scalar(sci[:, 1:2], sci[:, 0:1], 1, None, ALU.logical_shift_right))
                        step(v.tensor_copy(sc[:, 0:1], cnt))
                        step(v.tensor_tensor(sc[:, 1:2], sc[:, 0:1], sci[:, 1:2], ALU.subtract))
                        step(v.tensor_scalar(sc[:, 2:3], sc[:, 1:2], 2.0, None, ALU.mult))
                        step(v.tensor_scalar(sc[:, 3:4], sc[:, 0:1], 5.0, None, ALU.is_gt))
                        step(v.scalar_tensor_tensor(out=nb, in0=rk_, scalar=sc[:, 1:2], in1=nb, op0=ALU.not_equal,
                                                    op1=ALU.mult))
                        step(v.scalar_tensor_tensor(out=nb, in0=rk_, scalar=sc[:, 2:3], in1=nb, op0=ALU.not_equal,
                                                    op1=ALU.mult))
                        step(v.tensor_scalar(nb, nb, sc[:, 3:4], None, ALU.mult))
                        step(v.tensor_reduce(sc[:, 4:5], nb, AX.X, ALU.add))
                        step(v.tensor_tensor(vals[:, 0:N], xT, nb, ALU.mult))
                        step(v.tensor_scalar(nb, nb, -1.0, BIG, ALU.add, ALU.mult))
                        step(v.tensor_tensor(vals[:, 0:N], vals[:, 0:N], nb, ALU.add))
                        step(v.tensor_copy(sci[:, 2:3], sc[:, 4:5]))
                        n_kept = dve.value_load(sci[0:1, 2:3], min_val=0, max_val=N)
                        done = steps[0]
                        with dve.Fori(0, NP // 8) as j:
                            with dve.If(n_kept > j * 8):
                                restart()
                                step(v.max(top8[:], vals[:, 0:N]))
                                step(v.tensor_copy(ranked[:, bass.ds(j * 8, 8)], top8[:]))
                                step(v.match_replace(vals[:, 0:N], top8[:], vals[:, 0:N], -BIG))
                        restart()
                        for q, (mul, add, shift) in enumerate(((1.0, 3.0, 2), (1.0, 1.0, 1), (3.0, 3.0, 2))):
                            step(v.tensor_scalar(sci[:, 3:4], sc[:, 4:5], mul, add, ALU.mult, ALU.add))
                            step(v.tensor_scalar(sci[:, 4:5], sci[:, 3:4], shift, None, ALU.logical_shift_right))
                            step(v.tensor_scalar(sc[:, 5:6], sci[:, 4:5], 1.0, None, ALU.max))
                            step(v.tensor_tensor(sc[:, 6:7], sc[:, 4:5], sc[:, 5:6], ALU.subtract))
                            step(v.scalar_tensor_tensor(out=nbr, in0=col_no[:], scalar=sc[:, 6:7], in1=ranked[:],
                                                        op0=ALU.is_equal, op1=ALU.mult))
                            step(v.tensor_reduce(sc[:, 8 + q:9 + q], nbr, AX.X, ALU.add))
                        step(v.tensor_scalar(sc[:, 12:13], sc[:, 8:9], THIRD_HALF, None, ALU.mult))
                        step(v.scalar_tensor_tensor(out=sc[:, 13:14], in0=sc[:, 9:10], scalar=THIRD_HALF,
                                                    in1=sc[:, 12:13], op0=ALU.mult, op1=ALU.add))
                        step(v.scalar_tensor_tensor(out=sc[:, 14:15], in0=sc[:, 10:11], scalar=THIRD_HALF,
                                                    in1=sc[:, 13:14], op0=ALU.mult, op1=ALU.add))
                        v.scalar_tensor_tensor(out=comb_col[:], in0=x_col[:], scalar=0.5, in1=sc[:, 14:15],
                                               op0=ALU.mult, op1=ALU.add).then_inc(s_rc, 1)
                        dve.wait_ge(s_rp, 1)
                        dve.sem_clear(s_rp)
                        step(v.tensor_tensor(sc[:, 16:17], ps_out[:, 0:1], b_col[:], ALU.add))
                        v.tensor_tensor(out_col[:], sc[:, 16:17], x_col[:], ALU.add).then_inc(s_ro, 1)


_INS = ["x", "adj", "L0_gnn_W", "L0_gnn_b"]


def kernel(**inputs):
    import concourse.bacc as bacc
    from concourse.bass_utils import run_bass_kernel_spmd as run

    nc = bacc.Bacc("TRN2", target_bir_lowering=False, num_devices=1)
    arrays, args = {}, []
    for name in _INS:
        a = np.ascontiguousarray(inputs[name])
        arrays[f"in_{name}"] = a
        args.append(nc.dram_tensor(f"in_{name}", a.shape, mybir.dt.from_np(a.dtype), kind="ExternalInput").ap())
    rows, feats = arrays["in_x"].shape
    args.append(nc.dram_tensor("flag_rows", (rows,), I32, kind="Internal").ap())
    args.append(nc.dram_tensor("out_0", (rows, feats), F32, kind="ExternalOutput").ap())
    build(nc, *args)
    r = run(nc, [arrays], core_ids=[0])
    return r.results[0]["out_0"]
```

```python
from contextlib import ExitStack

import concourse.bass as bass
import numpy as np
from concourse import mybir

F32 = mybir.dt.float32
BF16 = mybir.dt.bfloat16
I32 = mybir.dt.int32
U32 = mybir.dt.uint32
ALU = mybir.AluOpType
ACT = mybir.ActivationFunctionType
AX = mybir.AxisListType

P = 128
GT = 6
RING = 6
BANKS = 3
CHUNK = 3
BITS = 16
TOP = 16
LEVELS = 3
SLOTS = 12
MID = 32
BIG = float(np.finfo(np.float32).max)
NOROW = 8192
THIRD_HALF = float(np.float32(0.5) * np.float32(1.0 / 3.0))
EXPONENT = 0x7F800000


def build(nc, x, adj, W, b, flag_rows, out):
    N, D = x.shape
    assert D == P
    NW = -(-N // BITS)
    assert NW <= 256 and 8 + BITS <= 24
    NP = NW * BITS
    NT = -(-N // P)
    LAST = N - P
    NG = NT // GT
    TT = NT - NG * GT
    assert 0 < TT <= CHUNK and GT % CHUNK == 0 and GT == RING and GT % BANKS == 0 and NG >= 3
    NC = GT // CHUNK
    NF = (LEVELS + 1) * TOP + 3
    SUM = (LEVELS + 1) * TOP

    with ExitStack() as ctx:
        def sb(name, shape, dt):
            return ctx.enter_context(nc.sbuf_tensor(name, shape, dt))

        def psum(name, shape, dt=F32):
            return ctx.enter_context(nc.psum_tensor(name, shape, dt))

        def sem(name):
            return ctx.enter_context(nc.semaphore(name))

        adj_ring = [sb(f"adj{i}", [P, NP], I32) for i in range(RING)]
        sq_ring = sb("sq_ring", [P, RING, NP], BF16)
        x_grp = sb("x_grp", [P, GT, D], F32)
        w_in = sb("w_in", [P, D], F32)
        wT = sb("wT", [P, D], F32)
        b_row = sb("b_row", [1, D], F32)
        b_col = sb("b_col", [P, 1], F32)
        ident = sb("ident", [P, P], F32)
        half_ident = sb("half_ident", [P, P], F32)
        ident_bf = sb("ident_bf", [P, P], BF16)
        bit_diag = sb("bit_diag", [P, BITS, P], BF16)
        before = sb("before", [P, P], BF16)
        ones_bf = sb("ones_bf", [P, P], BF16)
        ones_f = sb("ones_f", [P, P], F32)
        word_no = sb("word_no", [1, NW], BF16)
        dest_no = sb("dest_no", [P, P], BF16)
        slot_no = sb("slot_no", [P, TOP], F32)
        row_code = sb("row_code", [P, NT, 2], F32)
        counts_here = sb("counts_here", [P, NT], F32)
        pads = sb("pads", [P, 2, D], F32)
        spread = sb("spread", [MID, 2, P], F32)
        own_slot = sb("own_slot", [P, 8], F32)
        mid_pads = sb("mid_pads", [P, D], F32)
        part_i = sb("part_i", [P, 1], I32)
        part_a = sb("part_a", [P, 1], I32)
        part_f = sb("part_f", [P, 2], F32)
        sign_f = sb("sign_f", [P, 1], F32)
        rest_words = sb("rest_words", [P, NW], F32)
        row_sum = sb("row_sum", [P, NT], F32)
        words = sb("words", [P, GT, TOP], I32)
        low_i = sb("low_i", [P, GT, TOP], I32)
        rest = sb("rest", [P, GT, TOP], F32)
        fields = sb("fields", [P, GT, NF], F32)
        present = sb("present", [P, GT, LEVELS * TOP], BF16)
        count = sb("count", [P, GT], F32)
        same = sb("same", [P, GT], F32)
        listed = sb("listed", [P, GT], F32)
        upto10 = sb("upto10", [P, GT], F32)
        slow = sb("slow", [P, NT], F32)
        flags = sb("flags", [P, 3, GT], BF16)
        mid_here = sb("mid_here", [P, 1], F32)
        mid_before = sb("mid_before", [P, 1], BF16)
        place = sb("place", [P, 3, GT], F32)
        hot = sb("hot", [P, 2, GT, P], BF16)
        hot_mid = sb("hot_mid", [P, GT, MID], BF16)
        hotT = sb("hotT", [P, 2, GT * P], F32)
        exponent = sb("exponent", [P, 2, LEVELS * TOP], I32)
        col_base = sb("col_base", [P, 2, TOP], F32)
        cand = sb("cand", [P, 2, LEVELS * TOP], F32)
        cand_rest = sb("cand_rest", [P, LEVELS * TOP], F32)
        top_a = sb("top_a", [P, 8], F32)
        top_b = sb("top_b", [P, TOP], F32)
        gone = sb("gone", [P, 2], F32)
        odd = sb("odd", [P, 1], F32)
        kept = sb("kept", [P, TOP], F32)
        keys = sb("keys", [P, SLOTS], F32)
        keys0 = sb("keys0", [P, SLOTS], F32)
        missing = sb("missing", [P, SLOTS], F32)
        idx = sb("idx", [P, SLOTS], U32)
        idx_tail = sb("idx_tail", [P, SLOTS], U32)
        w_low = sb("w_low", [P, 2, 2], F32)
        ga_all = sb("ga", [P, SLOTS, D], F32)
        ga_tail = sb("ga_tail", [P, SLOTS, D], F32)
        gb = sb("gb", [P, SLOTS, D], F32)
        agg = sb("agg", [P, 2, D], F32)
        combT = sb("combT", [P, CHUNK * P], F32)
        res = sb("res", [P, NC, CHUNK, D], F32)
        mid = sb("mid", [MID, NF], F32)
        mid_exp = sb("mid_exp", [MID, LEVELS * TOP], I32)
        mid_base = sb("mid_base", [MID, TOP], F32)
        mid_cand = sb("mid_cand", [MID, LEVELS * TOP], F32)
        mid_crest = sb("mid_crest", [MID, LEVELS * TOP], F32)
        mid_list = sb("mid_list", [MID, TOP], F32)
        mid_gone = sb("mid_gone", [MID, 3], F32)
        mid_kept = sb("mid_kept", [MID, TOP], F32)
        mid_rest = sb("mid_rest", [MID, TOP], F32)
        mid_top = sb("mid_top", [MID, TOP], F32)
        mid_miss = sb("mid_miss", [MID, TOP], F32)
        mid_row = sb("mid_row", [MID, 1], U32)
        mid_ndiag = sb("mid_ndiag", [MID, MID], F32)
        mid_sel = sb("mid_sel", [P, 4, 8], F32)
        mid_idxf = sb("mid_idxf", [P, 4], F32)
        mid_idx = sb("mid_idx", [P, 4], U32)
        mid_x = sb("mid_x", [MID, D], F32)
        mid_g = sb("mid_g", [P, 4, D], F32)
        mid_s = sb("mid_s", [P, 2, TOP, MID], F32)
        mid_w = sb("mid_w", [P, 4, MID], F32)
        mid_t = sb("mid_t", [P, 2, MID], F32)
        mid_out = sb("mid_out", [MID, D], F32)
        slow_i = sb("slow_i", [P, NT], I32)
        slow_sum = sb("slow_sum", [P, 1], F32)
        slow_n = sb("slow_n", [P, 1], I32)
        top8 = sb("top8", [P, 8], F32)
        sc = sb("sc", [P, 24], F32)
        sci = sb("sci", [P, 8], I32)
        x_col = sb("x_col", [P, 1], F32)
        comb_col = sb("comb_col", [P, 1], F32)
        out_col = sb("out_col", [P, 1], F32)
        a_row = adj_ring[0]
        nbr = adj_ring[1][:].bitcast(F32)
        rank = adj_ring[2][:].bitcast(F32)
        vals = adj_ring[3][:].bitcast(F32)
        ranked = adj_ring[4][:].bitcast(F32)
        slow_row = adj_ring[5][0:1, 0:N]
        xT = sq_ring[:].rearrange("p r n -> p (r n)").bitcast(F32)[:, 0:N]

        ps_words = [psum(f"ps_words{i}", [P, 512]) for i in range(BANKS)]
        ps_small = psum("ps_small", [P, 512])
        ps_hotT = psum("ps_hotT", [P, 1024], BF16)
        ps_comb = psum("ps_comb", [P, 512])
        ps_out = psum("ps_out", [P, 512])
        ps_mT = psum("ps_mT", [P, 512])
        ps_place = ps_small[:, 0:3 * GT].rearrange("p (c t) -> p c t", c=3)
        ps_bl = ps_small[:, 32:32 + 2 * (SUM + 1)].rearrange("p (c f) -> p c f", c=2)
        ps_mid = ps_small[0:MID, 256:256 + NF]
        high = fields[:].rearrange("p t f -> p (t f)").bitcast(BF16).rearrange(
            "p (t f h) -> p t f h", f=NF, h=2)[:, :, :, 1]

        s_x = sem("x_loaded")
        s_wb = sem("weights_loaded")
        s_adj = [sem(f"adj_loaded{i}") for i in range(RING)]
        s_pool_step = sem("pool_step")
        s_const = sem("pool_constants_ready")
        s_vconst = sem("vector_constants_ready")
        s_wps = sem("w_transposed")
        s_wT = sem("wT_ready")
        s_sq = sem("adj_squared")
        s_words = sem("words_packed")
        s_top = sem("words_listed")
        s_flags = sem("flags_ready")
        s_place = sem("places_counted")
        s_hot = sem("hot_ready")
        s_comp = sem("blocks_filled")
        s_idx = sem("indices_ready")
        s_pads = sem("pads_written")
        s_go = sem("gathers_issued")
        s_gath = sem("rows_gathered")
        s_gath_tail = sem("tail_rows_gathered")
        s_agg = sem("agg_ready")
        s_hps = sem("hotT_in_psum")
        s_hT = sem("hotT_copied")
        s_cps = sem("comb_in_psum")
        s_comb = sem("comb_copied")
        s_ops = sem("out_in_psum")
        s_res = sem("result_ready")
        s_wr = sem("result_written")
        s_step = sem("vector_step")
        s_passed = sem("vector_past_wait")
        s_mpads = sem("mid_pads_written")
        s_mkeys = sem("mid_keys_ready")
        s_mspread = sem("mid_keys_spread")
        s_midx = sem("mid_indices_ready")
        s_mgath = sem("mid_rows_gathered")
        s_mT = sem("mid_transposed")
        s_mS = sem("mid_sorted_layout_ready")
        s_mxT = sem("mid_x_transposed")
        s_mcomb = sem("mid_comb_ready")
        s_mops = sem("mid_out_in_psum")
        s_mres = sem("mid_result_ready")
        s_mwr = sem("mid_written")
        s_slsum = sem("slow_summed")
        s_slps = sem("slow_total_in_psum")
        s_sln = sem("slow_count_ready")
        s_slsc = sem("slow_scratch_written")
        s_slin = sem("slow_inputs_loaded")
        s_ra = sem("slow_row_loaded")
        s_rc = sem("slow_comb_ready")
        s_rp = sem("slow_out_in_psum")
        s_ro = sem("slow_result_ready")
        s_rw = sem("slow_row_written")

        block = ctx.enter_context(nc.Block())

        def groups(eng, front):
            front(0, GT, 0)
            front(1, GT, 1)
            with eng.Fori(2, NG) as g:
                front(g, GT, 2)
            front(NG, TT, 2)

        @block.sync
        def _(sp):
            def load(g, i, wait):
                if wait:
                    sp.wait_ge(s_sq, g * GT + (i + 1 - RING))
                t = g * GT + i
                src = adj[LAST:N, :] if isinstance(g, int) and t == NT - 1 else adj[bass.ds(t * P, P), :]
                sp.dma_start(adj_ring[i % RING][:, 0:N], src).then_inc(s_adj[i % RING], 16)

            def front(g, tiles, older):
                for i in range(tiles):
                    load(g, i, wait=older > 0)
                    if older == 0 and i == 0:
                        sp.dma_start(w_in[:], W).then_inc(s_wb, 16)
                        sp.dma_start(b_row[:], b.rearrange("(a d) -> a d", a=1)).then_inc(s_wb, 16)
                        sp.dma_start(b_col[:], b.rearrange("(d a) -> d a", a=1)).then_inc(s_wb, 16)

            groups(sp, front)

            sp.wait_ge(s_sln, 1)
            n_slow = sp.value_load(slow_n[0:1, 0:1], min_val=0, max_val=N)
            with sp.If(n_slow > 0):
                sp.dma_start(flag_rows[0:(NT - 1) * P].rearrange("(t p) -> p t", p=P),
                             slow_i[:, 0:NT - 1], allow_slow_non_contiguous=True).then_inc(s_slsc, 16)
                sp.dma_start(flag_rows[(NT - 1) * P:N].rearrange("(p a) -> p a", a=1),
                             slow_i[NT * P - N:P, NT - 1:NT], allow_slow_non_contiguous=True).then_inc(s_slsc, 16)
                sp.wait_ge(s_mwr, 16)
                sp.wait_ge(s_slsc, 32)
                sp.dma_start(slow_row, flag_rows.rearrange("(a n) -> a n", a=1)).then_inc(s_slin, 16)
                sp.dma_start(xT, x.rearrange("n d -> d n"), allow_slow_non_contiguous=True).then_inc(s_slin, 16)
                sp.wait_ge(s_slin, 32)
                with sp.Fori(0, N) as r:
                    is_slow = sp.value_load(slow_row[0:1, bass.ds(r, 1)], min_val=0, max_val=1)
                    with sp.If(is_slow > 0):
                        sp.dma_start(a_row[:, 0:N], adj[bass.ds(r, 1), :].broadcast_to([P, N])).then_inc(s_ra, 16)
                        sp.wait_ge(s_ro, 1)
                        sp.sem_clear(s_ro)
                        sp.dma_start(out[bass.ds(r, 1), :].rearrange("a d -> d a"), out_col[:],
                                     allow_slow_non_contiguous=True).then_inc(s_rw, 16)
                        sp.wait_ge(s_rw, 16)
                        sp.sem_clear(s_rw)

        @block.gpsimd
        def _(pool):
            steps = [0]

            def step(ins):
                steps[0] += 1
                ins.then_inc(s_pool_step, 1)
                pool.wait_ge(s_pool_step, steps[0])

            step(nc.gpsimd.memset(ident[:], 0.0))
            step(nc.gpsimd.affine_select(out=ident[:], in_=ident[:], compare_op=ALU.not_equal, fill=1.0, base=0,
                                         pattern=[[-1, P]], channel_multiplier=1))
            step(nc.gpsimd.memset(ones_bf[:], 1.0))
            step(nc.gpsimd.affine_select(out=before[:], in_=ones_bf[:], compare_op=ALU.is_gt, fill=0.0, base=0,
                                         pattern=[[1, P]], channel_multiplier=-1))
            step(nc.gpsimd.iota(word_no[:], [[1, NW]], base=0, channel_multiplier=0,
                                allow_small_or_imprecise_dtypes=True))
            nc.gpsimd.memset(ones_f[:], 1.0).then_inc(s_const, 1)
            step(nc.gpsimd.iota(dest_no[:], [[1, P]], base=1, channel_multiplier=0,
                                allow_small_or_imprecise_dtypes=True))
            step(nc.gpsimd.iota(slot_no[:], [[1, TOP]], base=0, channel_multiplier=0,
                                allow_small_or_imprecise_dtypes=True))
            step(nc.gpsimd.iota(row_code[:, :, 0], [[P, NT]], base=-NOROW, channel_multiplier=0,
                                allow_small_or_imprecise_dtypes=True))
            step(nc.gpsimd.iota(row_code[:, NT - 1:NT, 0], [[0, 1]], base=LAST // 64 * 64 - NOROW,
                                channel_multiplier=0, allow_small_or_imprecise_dtypes=True))
            step(nc.gpsimd.iota(row_code[:, :, 1], [[0, NT]], base=0, channel_multiplier=1,
                                allow_small_or_imprecise_dtypes=True))
            step(nc.gpsimd.iota(row_code[:, NT - 1:NT, 1], [[0, 1]], base=LAST % 64, channel_multiplier=1,
                                allow_small_or_imprecise_dtypes=True))
            step(nc.gpsimd.memset(counts_here[:], 1.0))
            step(nc.gpsimd.memset(counts_here[0:NT * P - N, NT - 1:NT], 0.0))
            step(nc.gpsimd.memset(pads[:, 0, :], -BIG))
            step(nc.gpsimd.memset(pads[:, 1, :], BIG))
            step(nc.gpsimd.memset(ga_all[:], 0.0))
            step(nc.gpsimd.memset(ga_tail[:], 0.0))
            step(nc.gpsimd.memset(gb[:], 0.0))
            step(nc.gpsimd.memset(mid_x[:], 0.0))
            step(nc.gpsimd.iota(spread[:], [[16, 2], [1, 16], [0, 8]], base=0, channel_multiplier=-1,
                                allow_small_or_imprecise_dtypes=True))
            nc.gpsimd.iota(part_i[:], [[0, 1]], base=0, channel_multiplier=1).then_inc(s_const, 1)

            def load_x(g, tiles):
                if tiles == GT:
                    pool.dma_start(x_grp[:], x[bass.ds(g * (GT * P), GT * P), :].rearrange("(t p) d -> p t d", p=P)
                                   ).then_inc(s_x, 16)
                else:
                    pool.dma_start(x_grp[:, 0:TT - 1, :],
                                   x[NG * GT * P:(NT - 1) * P, :].rearrange("(t p) d -> p t d", p=P)).then_inc(s_x, 16)
                    pool.dma_start(x_grp[:, TT - 1, :], x[LAST:N, :]).then_inc(s_x, 16)

            def back(g, tiles):
                for c in range(-(-tiles // CHUNK)):
                    pool.wait_ge(s_res, g * NC + (c + 1))
                    pool.sem_inc(s_go, 1)
                    n = min(CHUNK, tiles - c * CHUNK)
                    if tiles == GT:
                        rows = out[bass.ds(g * (GT * P) + c * CHUNK * P, n * P), :]
                        pool.dma_start(rows.rearrange("(t p) d -> p t d", p=P), res[:, c, 0:n, :]).then_inc(s_wr, 16)
                    else:
                        first = (NG * GT) * P
                        pool.dma_start(out[first:LAST + 1, :].rearrange("(t p) d -> p t d", p=P),
                                       res[:, 0, 0:TT - 1, :]).then_inc(s_wr, 16)
                        pool.dma_start(out[LAST + 1:LAST + 113, :], res[1:113, 0, TT - 1, :]).then_inc(s_wr, 16)
                        pool.dma_start(out[LAST + 113:N, :], res[113:P, 0, TT - 1, :]).then_inc(s_wr, 16)

            def front(g, tiles, older):
                if older == 2:
                    back(g - 2, GT)
                    load_x(g - 1, GT)
                tail = tiles < GT
                pool.wait_ge(s_idx, g + 1)
                pool.wait_ge(s_pads, g + 1)
                pool.sem_inc(s_go, 1)
                for s in range(SLOTS):
                    nc.gpsimd.indirect_dma_start(
                        (ga_tail if tail else ga_all)[:, s, :], None, x,
                        bass.IndirectOffsetOnAxis(ap=(idx_tail if tail else idx)[:, s:s + 1], axis=0),
                        bounds_check=N - 1, oob_is_err=False).then_inc(s_gath_tail if tail else s_gath, 16)

            load_x(0, GT)
            groups(pool, front)
            pool.wait_ge(s_midx, 1)
            nc.gpsimd.indirect_dma_start(mid_x[:], None, x, bass.IndirectOffsetOnAxis(ap=mid_row[:], axis=0),
                                         bounds_check=N - 1, oob_is_err=False).then_inc(s_mgath, 16)
            pool.wait_ge(s_midx, 2)
            pool.wait_ge(s_mpads, 1)
            for u in range(4):
                nc.gpsimd.indirect_dma_start(mid_g[:, u, :], None, x,
                                             bass.IndirectOffsetOnAxis(ap=mid_idx[:, u:u + 1], axis=0),
                                             bounds_check=N - 1, oob_is_err=False).then_inc(s_mgath, 16)
            back(NG - 1, GT)
            load_x(NG, TT)
            back(NG, TT)
            pool.wait_ge(s_mres, 1)
            pool.wait_ge(s_wr, 16 * (NG * NC + 3))
            nc.gpsimd.indirect_dma_start(out, bass.IndirectOffsetOnAxis(ap=mid_row[:], axis=0), mid_out[:], None,
                                         bounds_check=N - 1, oob_is_err=False).then_inc(s_mwr, 16)
            pool.wait_ge(s_mwr, 16)

        @block.scalar
        def _(act):
            def square(g, i, wait):
                act.wait_ge(s_adj[i % RING], g * 16 + 16)
                if wait:
                    act.wait_ge(s_words, g * GT + (i + 1 - RING))
                else:
                    act.wait_ge(s_vconst, 1)
                nc.scalar.activation(sq_ring[:, i % RING, :], adj_ring[i % RING][:], ACT.Square,
                                     accum_out=row_sum[:, bass.ds(g * GT + i, 1)]).then_inc(s_sq, 1)

            def hot_copies(g, tiles):
                for c in range(-(-tiles // CHUNK)):
                    n = min(CHUNK, tiles - c * CHUNK) * P
                    for k in range(2):
                        act.wait_ge(s_hps, g * (2 * NC) + (2 * c + k + 1))
                        if not isinstance(g, int) or g >= 1:
                            act.wait_ge(s_cps, g * NC)
                        nc.scalar.activation(hotT[:, k, c * CHUNK * P:c * CHUNK * P + n], ps_hotT[:, 0:n],
                                             ACT.Copy).then_inc(s_hT, 1)

            def comb_copy(g, tiles, c):
                n = min(CHUNK, tiles - c * CHUNK) * P
                act.wait_ge(s_cps, g * NC + (c + 1))
                if not (isinstance(g, int) and g == 0 and c == 0):
                    act.wait_ge(s_ops, g * NC + c)
                nc.scalar.activation(combT[:, 0:n], ps_comb[:, 0:n], ACT.Copy).then_inc(s_comb, 1)

            def comb_copies(g, tiles):
                for c in range(-(-tiles // CHUNK)):
                    comb_copy(g, tiles, c)

            def write_pads(g, tail=False):
                if tail:
                    nc.scalar.activation(ga_tail[:, SLOTS - 2:SLOTS, :], pads[:], ACT.Copy).then_inc(s_pads, 1)
                    return
                if not (isinstance(g, int) and g == 0):
                    act.wait_ge(s_agg, g)
                else:
                    act.wait_ge(s_const, 2)
                nc.scalar.activation(ga_all[:, SLOTS - 2:SLOTS, :], pads[:], ACT.Copy).then_inc(s_pads, 1)

            def front(g, tiles, older):
                for i in range(tiles):
                    square(g, i, wait=older > 0)
                    if older == 0 and i == 0:
                        act.wait_ge(s_wps, 1)
                        nc.scalar.activation(wT[:], ps_comb[:, 0:D], ACT.Copy).then_inc(s_wT, 1)
                    if older and i == 1:
                        write_pads(g - 1)
                    if older == 2 and tiles == GT and i in (2, 3):
                        comb_copy(g - 2, GT, i - 2)
                    if older and tiles == GT and i == tiles - 1:
                        hot_copies(g - 1, GT)
                if tiles < GT:
                    comb_copies(g - 2, GT)
                    hot_copies(g - 1, GT)

            groups(act, front)
            write_pads(NG, tail=True)
            for u in range(4):
                last = nc.scalar.activation(mid_g[:, u, :], mid_pads[:], ACT.Copy)
            last.then_inc(s_mpads, 1)
            comb_copies(NG - 1, GT)
            hot_copies(NG, TT)
            comb_copies(NG, TT)
            act.wait_ge(s_mT, 1)
            for u in range(4):
                h, sh = u // 2, u % 2
                last = nc.scalar.activation(mid_s[:, 0, sh * 8:sh * 8 + 8, h * 16:h * 16 + 16],
                                            ps_mT[:, u * P:(u + 1) * P].rearrange("p (b s) -> p s b", s=8), ACT.Copy)
            last.then_inc(s_mS, 1)

        @block.tensor
        def _(pe):
            pe.wait_ge(s_const, 1)
            pe.wait_ge(s_wb, 48)
            nc.tensor.transpose(ps_comb[:, 0:D], w_in[:], ident[:]).then_inc(s_wps, 1)
            pe.wait_ge(s_vconst, 1)

            def pack(g, i, wait):
                pe.wait_ge(s_sq, g * GT + (i + 1))
                if wait:
                    pe.wait_ge(s_top, g * GT + (i + 1 - BANKS))
                bank = ps_words[i % BANKS][:, 0:NW]
                nc.tensor.matmul(bank, ones_bf[0:1, :], word_no[0:1, :], start=True, stop=False)
                for k in range(BITS):
                    last = nc.tensor.matmul(bank, bit_diag[:, k, :], sq_ring[:, i % RING, k * NW:(k + 1) * NW],
                                            start=False, stop=(k == BITS - 1))
                last.then_inc(s_words, 1)

            def turn_hot(g, tiles):
                for c in range(-(-tiles // CHUNK)):
                    for k in range(2):
                        n = min(CHUNK, tiles - c * CHUNK)
                        pe.wait_ge(s_hot, g + 1)
                        if not (isinstance(g, int) and g == 0 and c == 0 and k == 0):
                            pe.wait_ge(s_hT, g * (2 * NC) + (2 * c + k))
                        for i in range(n):
                            last = nc.tensor.transpose(ps_hotT[:, i * P:(i + 1) * P], hot[:, k, c * CHUNK + i, :],
                                                       ident_bf[:])
                        last.then_inc(s_hps, 1)

            def combine(g, tiles, c, n):
                pe.wait_ge(s_agg, g + 1)
                pe.wait_ge(s_hT, g * (2 * NC) + (2 * c + 2))
                pe.wait_ge(s_x, g * 16 + (16 if tiles == GT else 32))
                if isinstance(g, int) and g == 0 and c == 0:
                    pe.wait_ge(s_wT, 1)
                else:
                    pe.wait_ge(s_comb, g * NC + c)
                for k in range(2):
                    nc.tensor.matmul(ps_comb[:, 0:n * P], agg[:, k, :], hotT[:, k, c * CHUNK * P:(c * CHUNK + n) * P],
                                     start=(k == 0), stop=False)
                for i in range(n):
                    last = nc.tensor.matmul(ps_comb[:, i * P:(i + 1) * P], x_grp[:, c * CHUNK + i, :],
                                            half_ident[:], start=False, stop=(i == n - 1))
                last.then_inc(s_cps, 1)

            def project(g, c, n):
                pe.wait_ge(s_comb, g * NC + (c + 1))
                if not (isinstance(g, int) and g == 0 and c == 0):
                    pe.wait_ge(s_res, g * NC + c)
                for i in range(n):
                    nc.tensor.matmul(ps_out[:, i * P:(i + 1) * P], combT[:, i * P:(i + 1) * P], wT[:],
                                     start=True, stop=False)
                    last = nc.tensor.matmul(ps_out[:, i * P:(i + 1) * P], ones_f[0:1, :], b_row[:],
                                            start=False, stop=True)
                last.then_inc(s_ops, 1)

            def dense(g, tiles):
                for c in range(-(-tiles // CHUNK)):
                    if c:
                        project(g, c - 1, CHUNK)
                    combine(g, tiles, c, min(CHUNK, tiles - c * CHUNK))

            def dense_end(g, tiles):
                c = -(-tiles // CHUNK) - 1
                project(g, c, tiles - c * CHUNK)

            def places(g, tiles):
                pe.wait_ge(s_flags, g + 1)
                nc.tensor.matmul(ps_place[:, :, 0:tiles], before[:], flags[:, :, 0:tiles], start=True, stop=False)
                for d in range(1, tiles):
                    nc.tensor.matmul(ps_place[:, :, d:tiles], ones_bf[:], flags[:, :, 0:tiles - d],
                                     start=False, stop=False)
                for i in range(tiles):
                    last = nc.tensor.matmul(ps_place[:, 2, i:i + 1], ones_bf[:], mid_before[:], start=False,
                                            stop=(i == tiles - 1))
                last.then_inc(s_place, 1)

            def fill_blocks(g, tiles):
                pe.wait_ge(s_hot, g + 1)
                for k in range(2):
                    for i in range(tiles):
                        nc.tensor.matmul(ps_bl[:, k, :], hot[:, k, i, :], high[:, i, 0:SUM + 1],
                                         start=(i == 0), stop=(i == tiles - 1))
                for i in range(tiles):
                    last = nc.tensor.matmul(ps_mid, hot_mid[:, i, :], high[:, i, :], start=(i == 0),
                                            stop=(i == tiles - 1))
                last.then_inc(s_comp, 1)

            def front(g, tiles, older):
                for i in range(tiles):
                    pack(g, i, wait=older > 0 or i >= BANKS)
                    if older == 2 and tiles == GT:
                        if i == 1:
                            combine(g - 2, GT, 0, CHUNK)
                        if i == 2:
                            project(g - 2, 0, CHUNK)
                            combine(g - 2, GT, 1, CHUNK)
                        if i == 3:
                            project(g - 2, 1, CHUNK)
                    if older and tiles == GT and i == 4:
                        turn_hot(g - 1, GT)
                if tiles < GT:
                    dense(g - 2, GT)
                    dense_end(g - 2, GT)
                    turn_hot(g - 1, GT)
                places(g, tiles)
                fill_blocks(g, tiles)

            groups(pe, front)
            pe.wait_ge(s_mkeys, 1)
            for h in range(2):
                nc.tensor.matmul(ps_words[0][:, h * TOP:(h + 1) * TOP], spread[:, h, :], mid_top[:],
                                 start=True, stop=True)
            nc.tensor.matmul(ps_words[0][:, 64:64 + MID], ones_f[0:MID, :], mid_ndiag[:], start=True,
                             stop=True).then_inc(s_mspread, 1)
            dense(NG - 1, GT)
            turn_hot(NG, TT)
            dense_end(NG - 1, GT)
            dense(NG, TT)
            dense_end(NG, TT)
            pe.wait_ge(s_mgath, 16 * 5)
            for u in range(4):
                last = nc.tensor.transpose(ps_mT[:, u * P:(u + 1) * P], mid_g[:, u, :], ident[:])
            last.then_inc(s_mT, 1)
            nc.tensor.matmul(ps_words[1][:, 0:MID], mid_x[:], half_ident[0:MID, 0:MID], start=True,
                             stop=True).then_inc(s_mxT, 1)
            pe.wait_ge(s_mcomb, 1)
            nc.tensor.matmul(ps_words[2][0:MID, 0:D], mid_t[:, 1, :], wT[:], start=True, stop=False)
            nc.tensor.matmul(ps_words[2][0:MID, 0:D], ones_f[0:1, 0:MID], b_row[:], start=False,
                             stop=True).then_inc(s_mops, 1)
            pe.wait_ge(s_slsum, 1)
            nc.tensor.matmul(ps_small[:, 0:1], ones_f[:], slow_sum[:], start=True, stop=True).then_inc(s_slps, 1)
            pe.wait_ge(s_sln, 1)
            n_slow = pe.value_load(slow_n[0:1, 0:1], min_val=0, max_val=N)
            with pe.If(n_slow > 0):
                pe.wait_ge(s_slin, 32)
                with pe.Fori(0, N) as r:
                    is_slow = pe.value_load(slow_row[0:1, bass.ds(r, 1)], min_val=0, max_val=1)
                    with pe.If(is_slow > 0):
                        pe.wait_ge(s_rc, 1)
                        pe.sem_clear(s_rc)
                        nc.tensor.matmul(ps_out[:, 0:1], wT[:], comb_col[:], start=True, stop=True).then_inc(s_rp, 1)

        @block.vector
        def _(dve):
            v = nc.vector
            steps = [0]

            def step(ins):
                steps[0] += 1
                ins.then_inc(s_step, 1)
                dve.wait_ge(s_step, steps[0])

            def restart():
                dve.sem_clear(s_step)
                steps[0] = 0

            def did(ins):
                steps[0] += 1
                ins.then_inc(s_step, 1)
                return steps[0]

            def need(n):
                dve.wait_ge(s_step, n)

            for i in range(RING):
                step(v.memset(adj_ring[i][:, N:NP], 0))
            step(v.memset(mid[:], 0.0))
            step(v.memset(mid_before[:], 0.0))
            step(v.memset(slow[:], 0.0))
            step(v.memset(fields[:], 0.0))
            dve.wait_ge(s_const, 1)
            step(v.tensor_copy(ident_bf[:], ident[:]))
            step(v.tensor_scalar(half_ident[:], ident[:], 0.5, None, ALU.mult))
            for k in range(BITS):
                last = v.tensor_scalar(bit_diag[:, k, :], ident_bf[:], float(2 ** (k + 8)), None, ALU.mult)
            last.then_inc(s_vconst, 1)
            dve.wait_ge(s_const, 2)
            step(v.tensor_scalar(spread[:], spread[:], 0.0, None, ALU.is_equal))
            step(v.tensor_scalar(part_a[:], part_i[:], 7, None, ALU.bitwise_and))
            step(v.tensor_copy(part_f[:, 0:1], part_a[:]))
            step(v.tensor_scalar(part_a[:], part_i[:], 1, None, ALU.bitwise_and))
            step(v.tensor_copy(part_f[:, 1:2], part_a[:]))
            step(v.tensor_scalar(own_slot[:], slot_no[:, 0:8], part_f[:, 0:1], None, ALU.is_equal))
            step(v.tensor_scalar(sign_f[:], part_f[:, 1:2], 2.0, -1.0, ALU.mult, ALU.add))
            step(v.tensor_scalar(mid_pads[:], pads[:, 1, :], sign_f[:, 0:1], None, ALU.mult))

            def list_words(g, i):
                dve.wait_ge(s_words, g * GT + (i + 1))
                dve.sem_inc(s_passed, 1)
                bank = ps_words[i % BANKS][:, 0:NW]
                step(v.max(words[:, i, 0:8], bank))
                step(v.match_replace(rest_words[:], words[:, i, 0:8], bank, -1.0))
                v.max(words[:, i, 8:16], rest_words[:]).then_inc(s_top, 1)

            def decode(g, tiles):
                w, lo, rs = words[:, 0:tiles, :], low_i[:, 0:tiles, :], rest[:, 0:tiles, :]
                level = [fields[:, 0:tiles, l * TOP:(l + 1) * TOP] for l in range(LEVELS)]
                total = fields[:, 0:tiles, SUM]
                here = counts_here[:, bass.ds(g * GT, tiles)]
                dve.wait_ge(s_top, g * GT + tiles)
                step(v.tensor_scalar(lo, w, 255, None, ALU.bitwise_and))
                step(v.tensor_tensor(rs, w, lo, ALU.subtract))
                did(v.tensor_copy(fields[:, 0:tiles, LEVELS * TOP:SUM], lo))
                for l in range(LEVELS):
                    top = did(v.tensor_scalar(level[l].bitcast(I32), rs.bitcast(I32), EXPONENT, None,
                                              ALU.bitwise_and))
                    if l == 0:
                        did(v.tensor_tensor(total, row_sum[:, bass.ds(g * GT, tiles)], here, ALU.mult))
                    if l == 1:
                        did(v.tensor_copy(fields[:, 0:tiles, SUM + 1:SUM + 3], row_code[:, bass.ds(g * GT, tiles), :]))
                    need(top)
                    if l < LEVELS - 1:
                        step(v.tensor_tensor(rs, rs, level[l], ALU.subtract))
                step(v.tensor_scalar(present[:, 0:tiles, :], fields[:, 0:tiles, 0:LEVELS * TOP], 0.0, None, ALU.is_gt))
                n = count[:, 0:tiles]
                step(v.tensor_reduce(n, present[:, 0:tiles, :], AX.X, ALU.add))
                sm, li, up = same[:, 0:tiles], listed[:, 0:tiles], upto10[:, 0:tiles]
                step(v.tensor_tensor(sm, n, total, ALU.is_equal))
                step(v.scalar_tensor_tensor(out=li, in0=n, scalar=15.0, in1=sm, op0=ALU.is_le, op1=ALU.mult))
                step(v.scalar_tensor_tensor(out=li, in0=n, scalar=6.0, in1=li, op0=ALU.is_ge, op1=ALU.mult))
                did(v.scalar_tensor_tensor(out=slow[:, bass.ds(g * GT, tiles)], in0=total, scalar=6.0, in1=li,
                                           op0=ALU.is_ge, op1=ALU.subtract))
                did(v.scalar_tensor_tensor(out=flags[:, 0, 0:tiles], in0=n, scalar=6.0, in1=li,
                                           op0=ALU.is_le, op1=ALU.mult))
                step(v.scalar_tensor_tensor(out=up, in0=n, scalar=10.0, in1=li, op0=ALU.is_le, op1=ALU.mult))
                did(v.tensor_tensor(flags[:, 1, 0:tiles], up, flags[:, 0, 0:tiles], ALU.subtract))
                v.tensor_tensor(flags[:, 2, 0:tiles], li, up, ALU.subtract).then_inc(s_flags, 1)

            def assign(g, tiles):
                dve.wait_ge(s_place, g + 1)
                pl = place[:, :, 0:tiles]
                step(v.scalar_tensor_tensor(out=pl, in0=ps_place[:, :, 0:tiles], scalar=1.0,
                                            in1=flags[:, :, 0:tiles], op0=ALU.add, op1=ALU.mult))
                if not isinstance(g, int) or g > 0:
                    dve.wait_ge(s_hps, g * (2 * NC))
                for k in range(2):
                    for i in range(tiles):
                        v.tensor_scalar(hot[:, k, i, :], dest_no[:], place[:, k, i:i + 1], None, ALU.is_equal)
                for i in range(tiles):
                    last = v.tensor_scalar(hot_mid[:, i, :], dest_no[:, 0:MID], place[:, 2, i:i + 1], None,
                                           ALU.is_equal)
                last.then_inc(s_hot, 1)
                here = did(v.tensor_reduce(mid_here[:], flags[:, 2, 0:tiles], AX.X, ALU.add))
                sl = slow[:, bass.ds(g * GT, tiles)]
                step(v.scalar_tensor_tensor(out=sl, in0=place[:, 0, 0:tiles], scalar=float(P), in1=sl,
                                            op0=ALU.is_gt, op1=ALU.max))
                did(v.tensor_tensor(mid_before[:], mid_before[:], mid_here[:], ALU.add))
                step(v.scalar_tensor_tensor(out=sl, in0=place[:, 1, 0:tiles], scalar=float(P), in1=sl,
                                            op0=ALU.is_gt, op1=ALU.max))
                step(v.scalar_tensor_tensor(out=sl, in0=place[:, 2, 0:tiles], scalar=float(MID), in1=sl,
                                            op0=ALU.is_gt, op1=ALU.max))

            def columns(ex, base, cd, hb, number):
                did(v.tensor_scalar(ex, hb.bitcast(I32), 23, None, ALU.logical_shift_right))
                step(v.tensor_scalar(base, number, float(1 - NW * (127 + 8)), None, ALU.add))
                return did(v.scalar_tensor_tensor(
                    out=cd.rearrange("p (l t) -> p l t", t=TOP), in0=ex.rearrange("p (l t) -> p l t", t=TOP),
                    scalar=float(NW), in1=base.unsqueeze(1).broadcast_to([base.shape[0], LEVELS, TOP]),
                    op0=ALU.mult, op1=ALU.add))

            def block_indices(g, tail):
                dve.wait_ge(s_comp, g + 1)
                out_idx = idx_tail if tail else idx
                wl = w_low[:, int(tail), :]
                n = ps_bl[:, 1, SUM:SUM + 1]
                did(v.tensor_tensor(mid[:], mid[:], ps_mid, ALU.add))
                columns(exponent[:, 1, :], col_base[:, 1, :], cand[:, 1, :], ps_bl[:, 1, 0:LEVELS * TOP],
                        ps_bl[:, 1, LEVELS * TOP:SUM])
                both = columns(exponent[:, 0, :], col_base[:, 0, :], cand[:, 0, :], ps_bl[:, 0, 0:LEVELS * TOP],
                               ps_bl[:, 0, LEVELS * TOP:SUM])
                b8 = did(v.max(top_b[:, 0:8], cand[:, 1, :]))
                g0 = did(v.tensor_scalar(gone[:, 0:1], n, 8.0, 3.0, ALU.is_ge, ALU.add))
                need(b8)
                b_rest = did(v.match_replace(cand_rest[:], top_b[:, 0:8], cand[:, 1, :], -1e6))
                need(g0)
                g1 = did(v.scalar_tensor_tensor(out=gone[:, 1:2], in0=n, scalar=10.0, in1=gone[:, 0:1], op0=ALU.is_ge,
                                                op1=ALU.add))
                need(b_rest)
                b16 = did(v.max(top_b[:, 8:16], cand_rest[:]))
                need(both)
                a8 = did(v.max(top_a[:], cand[:, 0, :]))
                need(max(b16, g1))
                kp = did(v.scalar_tensor_tensor(out=kept[:], in0=slot_no[:], scalar=gone[:, 1:2], in1=top_b[:],
                                                op0=ALU.not_equal, op1=ALU.mult))
                od = did(v.scalar_tensor_tensor(out=odd[:], in0=gone[:, 1:2], scalar=-2.0, in1=n, op0=ALU.mult,
                                                op1=ALU.add))
                need(a8)
                ky = did(v.tensor_copy(keys[:, 0:4].rearrange("p (a c) -> p a c", a=2),
                                  top_a[:, 1:7].rearrange("p (a c) -> p a c", a=2)[:, :, 0:2]))
                need(max(kp, od))
                k0 = did(v.tensor_scalar(kept[:, 0:1], kept[:, 0:1], odd[:, 0:1], None, ALU.mult))
                did(v.tensor_scalar(wl[:, 0:1], n, 9.0, THIRD_HALF, ALU.is_ge, ALU.mult))
                need(k0)
                k8 = did(v.max(keys[:, 4:12], kept[:]))
                did(v.tensor_scalar(wl[:, 1:2], n, 9.0, THIRD_HALF, ALU.is_lt, ALU.mult))
                need(k8)
                step(v.tensor_scalar(keys0[:], keys[:], 0.0, -1.0, ALU.max, ALU.add))
                step(v.tensor_scalar(missing[:], keys[:], 0.0, float(NOROW + 1), ALU.is_le, ALU.mult))
                if not tail and (not isinstance(g, int) or g > 0):
                    dve.wait_ge(s_gath, g * (SLOTS * 16))
                v.tensor_tensor(out_idx[:], keys0[:], missing[:], ALU.add).then_inc(s_idx, 1)

            def low_high(dst_lo, dst_hi, a, c):
                if dst_lo is not None:
                    did(v.tensor_tensor(dst_lo, a, c, ALU.min))
                if dst_hi is not None:
                    did(v.tensor_tensor(dst_hi, a, c, ALU.max))

            def layer_done():
                dve.wait_ge(s_step, steps[0])

            def sort_and_pool(g, tail):
                if tail:
                    dve.wait_ge(s_gath_tail, SLOTS * 16)
                else:
                    dve.wait_ge(s_gath, g * (SLOTS * 16) + SLOTS * 16)
                ga = ga_tail if tail else ga_all
                wl = w_low[:, int(tail), :]
                pa = ga[:].rearrange("p (a c) d -> p a c d", c=2)
                pb = gb[:].rearrange("p (a c) d -> p a c d", c=2)
                low_high(pb[:, :, 0, :], pb[:, :, 1, :], pa[:, :, 0, :], pa[:, :, 1, :])
                layer_done()
                qa = ga[:].rearrange("p (q h c) d -> p q h (c d)", q=3, h=2)
                qb = gb[:].rearrange("p (q h c) d -> p q h (c d)", q=3, h=2)
                low_high(qa[:, :, 0, :], qa[:, :, 1, :], qb[:, :, 0, :], qb[:, :, 1, :])
                layer_done()
                la = ga[:].rearrange("p (q l) d -> p q l d", q=3)
                lb = gb[:].rearrange("p (q l) d -> p q l d", q=3)
                low_high(lb[:, :, 1, :], lb[:, :, 2, :], la[:, :, 1, :], la[:, :, 2, :])
                layer_done()
                A, B = ga[:, 4:12, :], gb[:, 4:12, :]
                low_high(None, B[:, 4, :], A[:, 0, :], A[:, 4, :])
                low_high(B[:, 3, :], None, A[:, 3, :], A[:, 7, :])
                low_high(A[:, 1:3, :], A[:, 5:7, :], B[:, 1:3, :], B[:, 5:7, :])
                layer_done()
                low_high(B[:, 2, :], A[:, 4, :], A[:, 2, :], B[:, 4, :])
                low_high(A[:, 3, :], B[:, 5, :], B[:, 3, :], A[:, 5, :])
                layer_done()
                low_high(B[:, 1, :], A[:, 2, :], A[:, 1, :], B[:, 2, :])
                low_high(B[:, 3, :], None, A[:, 3, :], A[:, 4, :])
                low_high(A[:, 5, :], None, B[:, 5, :], A[:, 6, :])
                layer_done()
                if not isinstance(g, int) or g > 0:
                    dve.wait_ge(s_cps, g * NC)
                a0, a1 = agg[:, 0, :], agg[:, 1, :]
                w = THIRD_HALF
                step(v.tensor_scalar(a0, ga[:, 0, :], w, None, ALU.mult))
                step(v.tensor_scalar(a1, B[:, 1, :], wl[:, 0:1], None, ALU.mult))
                step(v.scalar_tensor_tensor(out=a0, in0=gb[:, 1, :], scalar=w, in1=a0, op0=ALU.mult, op1=ALU.add))
                step(v.scalar_tensor_tensor(out=a1, in0=A[:, 2, :], scalar=wl[:, 1:2], in1=a1,
                                            op0=ALU.mult, op1=ALU.add))
                step(v.scalar_tensor_tensor(out=a0, in0=gb[:, 2, :], scalar=w, in1=a0, op0=ALU.mult, op1=ALU.add))
                step(v.scalar_tensor_tensor(out=a1, in0=B[:, 3, :], scalar=w, in1=a1, op0=ALU.mult, op1=ALU.add))
                v.scalar_tensor_tensor(out=a1, in0=A[:, 5, :], scalar=w, in1=a1, op0=ALU.mult,
                                       op1=ALU.add).then_inc(s_agg, 1)

            def add_self(g, tiles, c):
                n = min(CHUNK, tiles - c * CHUNK)
                dve.wait_ge(s_x, g * 16 + (16 if tiles == GT else 32))
                dve.wait_ge(s_ops, g * NC + (c + 1))
                if not isinstance(g, int) or g > 0:
                    dve.wait_ge(s_wr, g * (NC * 16))
                v.tensor_tensor(res[:, c, 0:n, :], ps_out[:, 0:n * P].rearrange("p (t d) -> p t d", d=D),
                                x_grp[:, c * CHUNK:c * CHUNK + n, :], ALU.add).then_inc(s_res, 1)

            def front(g, tiles, older):
                restart()
                for i in range(tiles):
                    list_words(g, i)
                    if older == 2 and tiles == GT and i in (2, 4):
                        add_self(g - 2, GT, i // 2 - 1)
                if tiles < GT:
                    add_self(g - 2, GT, 0)
                    add_self(g - 2, GT, 1)
                decode(g, tiles)
                if older and tiles == GT:
                    sort_and_pool(g - 1, False)
                assign(g, tiles)
                block_indices(g, tiles < GT)

            groups(dve, front)

            n = mid[:, SUM:SUM + 1]
            columns(mid_exp[:], mid_base[:], mid_cand[:], mid[:, 0:LEVELS * TOP], mid[:, LEVELS * TOP:SUM])
            layer_done()
            step(v.max(mid_list[:, 0:8], mid_cand[:]))
            step(v.match_replace(mid_crest[:], mid_list[:, 0:8], mid_cand[:], -1e6))
            step(v.max(mid_list[:, 8:16], mid_crest[:]))
            step(v.scalar_tensor_tensor(out=mid_row[:], in0=mid[:, SUM + 1:SUM + 2], scalar=float(NOROW),
                                        in1=mid[:, SUM + 2:SUM + 3], op0=ALU.add, op1=ALU.add))
            step(v.tensor_scalar(mid_gone[:, 0:1], n, 12.0, 5.0, ALU.is_ge, ALU.add))
            step(v.scalar_tensor_tensor(out=mid_gone[:, 1:2], in0=n, scalar=14.0, in1=mid_gone[:, 0:1], op0=ALU.is_ge,
                                        op1=ALU.add))
            step(v.scalar_tensor_tensor(out=mid_gone[:, 2:3], in0=mid_gone[:, 1:2], scalar=-2.0, in1=n, op0=ALU.mult,
                                        op1=ALU.add))
            step(v.scalar_tensor_tensor(out=mid_kept[:], in0=slot_no[0:MID, :], scalar=mid_gone[:, 1:2],
                                        in1=mid_list[:], op0=ALU.not_equal, op1=ALU.mult))
            step(v.tensor_scalar(mid_kept[:, 0:1], mid_kept[:, 0:1], mid_gone[:, 2:3], None, ALU.mult))
            step(v.max(mid_top[:, 0:8], mid_kept[:]))
            step(v.match_replace(mid_rest[:], mid_top[:, 0:8], mid_kept[:], -1e6))
            step(v.max(mid_top[:, 8:16], mid_rest[:]))
            step(v.tensor_scalar(mid_miss[:], mid_top[:], 0.0, float(NOROW + 1), ALU.is_le, ALU.mult))
            step(v.tensor_scalar(mid_top[:], mid_top[:], 0.0, -1.0, ALU.max, ALU.add))
            step(v.tensor_tensor(mid_top[:], mid_top[:], mid_miss[:], ALU.add))
            step(v.tensor_scalar(mid_ndiag[:], ident[0:MID, 0:MID], mid[:, SUM:SUM + 1], None, ALU.mult))
            v.tensor_reduce(slow_sum[:], slow[:], AX.X, ALU.add).then_inc(s_slsum, 1)
            v.tensor_scalar(slow_i[:], slow[:], 0.0, None, ALU.add).then_inc(s_mkeys, 1)
            dve.wait_ge(s_mkeys, 1)
            dve.sem_inc(s_midx, 1)
            dve.wait_ge(s_mspread, 1)
            spread_keys = ps_words[0][:, 0:2 * TOP].rearrange("p (u c) -> p u c", c=8)
            for u in range(4):
                last = v.tensor_tensor(mid_sel[:, u, :], spread_keys[:, u, :], own_slot[:], ALU.mult)
            step(last)
            step(v.tensor_reduce(mid_idxf[:], mid_sel[:], AX.X, ALU.add))
            v.tensor_copy(mid_idx[:], mid_idxf[:]).then_inc(s_midx, 1)
            n_all = ps_words[0][:, 64:64 + MID]
            for q, (edge, op) in enumerate(((13.0, ALU.is_ge), (13.0, ALU.is_lt), (15.0, ALU.is_lt), (15.0, ALU.is_ge))):
                step(v.tensor_scalar(mid_w[:, q, :], n_all, edge, THIRD_HALF, op, ALU.mult))

            sort_and_pool(NG - 1, False)
            sort_and_pool(NG, True)
            add_self(NG - 1, GT, 0)
            add_self(NG - 1, GT, 1)

            dve.wait_ge(s_mS, 1)
            home = [0]

            def lines(buf, start, groups_, gstep, run):
                a = mid_s[:, buf, :, :]
                if groups_ == 1:
                    return a[:, start:start + run, :]
                if run == 1:
                    return a[:, start:start + (groups_ - 1) * gstep + 1:gstep, :]
                end = start + groups_ * gstep
                if end <= TOP:
                    return a[:, start:end, :].rearrange("p (g r) m -> p g r m", g=groups_)[:, :, 0:run, :]
                lead = gstep - run
                return a[:, start - lead:start + (groups_ - 1) * gstep + run, :].rearrange(
                    "p (g r) m -> p g r m", g=groups_)[:, :, lead:gstep, :]

            def layer(pairs, copies):
                src, dst = home[0], 1 - home[0]
                for lo, hi, g_, st, run in pairs:
                    low_high(lines(dst, lo, g_, st, run), lines(dst, hi, g_, st, run),
                             lines(src, lo, g_, st, run), lines(src, hi, g_, st, run))
                for at, g_, st, run in copies:
                    v.tensor_copy(lines(dst, at, g_, st, run), lines(src, at, g_, st, run)).then_inc(s_step, 1)
                    steps[0] += 1
                layer_done()
                home[0] = dst

            layer([(0, 1, 8, 2, 1)], [])
            layer([(0, 2, 4, 4, 2)], [])
            layer([(1, 2, 4, 4, 1)], [(0, 4, 4, 1), (3, 4, 4, 1)])
            layer([(0, 4, 2, 8, 4)], [])
            layer([(2, 4, 1, 8, 2), (10, 12, 1, 8, 2)], [(0, 1, 1, 2), (6, 1, 1, 4), (14, 1, 1, 2)])
            layer([(1, 2, 3, 2, 1), (9, 10, 3, 2, 1)], [(0, 1, 1, 1), (7, 1, 1, 2), (15, 1, 1, 1)])
            layer([(0, 8, 1, 8, 8)], [])
            layer([(4, 8, 1, 4, 4)], [(2, 1, 1, 2), (12, 1, 1, 2)])
            layer([(2, 4, 3, 4, 2)], [])
            layer([(3, 4, 5, 2, 1)], [])
            rk = mid_s[:, home[0], :, :]
            t0, t1 = mid_t[:, 0, :], mid_t[:, 1, :]
            step(v.tensor_tensor(t1, rk[:, 4, :], mid_w[:, 0, :], ALU.mult))
            step(v.tensor_tensor(t0, rk[:, 5, :], mid_w[:, 1, :], ALU.mult))
            step(v.tensor_tensor(t1, t1, t0, ALU.add))
            step(v.scalar_tensor_tensor(out=t1, in0=rk[:, 7, :], scalar=THIRD_HALF, in1=t1, op0=ALU.mult, op1=ALU.add))
            for r_, q in ((10, 2), (11, 3)):
                step(v.tensor_tensor(t0, rk[:, r_, :], mid_w[:, q, :], ALU.mult))
                step(v.tensor_tensor(t1, t1, t0, ALU.add))
            dve.wait_ge(s_mxT, 1)
            v.tensor_tensor(t1, t1, ps_words[1][:, 0:MID], ALU.add).then_inc(s_mcomb, 1)

            add_self(NG, TT, 0)
            dve.wait_ge(s_mops, 1)
            v.tensor_tensor(mid_out[:], ps_words[2][0:MID, 0:D], mid_x[:], ALU.add).then_inc(s_mres, 1)
            dve.wait_ge(s_slps, 1)
            v.tensor_copy(slow_n[:], ps_small[:, 0:1]).then_inc(s_sln, 1)

            dve.wait_ge(s_sln, 1)
            n_slow = dve.value_load(slow_n[0:1, 0:1], min_val=0, max_val=N)
            with dve.If(n_slow > 0):
                restart()
                step(v.memset(ranked, 0.0))
                dve.wait_ge(s_slin, 32)
                with dve.Fori(0, N) as r:
                    is_slow = dve.value_load(slow_row[0:1, bass.ds(r, 1)], min_val=0, max_val=1)
                    with dve.If(is_slow > 0):
                        restart()
                        dve.wait_ge(s_ra, 16)
                        dve.sem_clear(s_ra)
                        step(v.tensor_copy(x_col[:], xT[:, bass.ds(r, 1)]))
                        nb, rk_ = nbr[:, 0:N], rank[:, 0:N]
                        step(v.tensor_scalar(nb, a_row[:, 0:N], 0.0, None, ALU.not_equal))
                        step(v.tensor_tensor_scan(rk_, nb, nb, 0.0, ALU.add, ALU.bypass))
                        cnt = rank[:, N - 1:N]
                        step(v.tensor_copy(sci[:, 0:1], cnt))
                        step(v.tensor_scalar(sci[:, 1:2], sci[:, 0:1], 1, None, ALU.logical_shift_right))
                        step(v.tensor_copy(sc[:, 0:1], cnt))
                        step(v.tensor_tensor(sc[:, 1:2], sc[:, 0:1], sci[:, 1:2], ALU.subtract))
                        step(v.tensor_scalar(sc[:, 2:3], sc[:, 1:2], 2.0, None, ALU.mult))
                        step(v.tensor_scalar(sc[:, 3:4], sc[:, 0:1], 5.0, None, ALU.is_gt))
                        step(v.scalar_tensor_tensor(out=nb, in0=rk_, scalar=sc[:, 1:2], in1=nb, op0=ALU.not_equal,
                                                    op1=ALU.mult))
                        step(v.scalar_tensor_tensor(out=nb, in0=rk_, scalar=sc[:, 2:3], in1=nb, op0=ALU.not_equal,
                                                    op1=ALU.mult))
                        step(v.tensor_scalar(nb, nb, sc[:, 3:4], None, ALU.mult))
                        step(v.tensor_reduce(sc[:, 4:5], nb, AX.X, ALU.add))
                        step(v.tensor_tensor(vals[:, 0:N], xT, nb, ALU.mult))
                        step(v.tensor_scalar(nb, nb, -1.0, BIG, ALU.add, ALU.mult))
                        step(v.tensor_tensor(vals[:, 0:N], vals[:, 0:N], nb, ALU.add))
                        step(v.tensor_copy(sci[:, 2:3], sc[:, 4:5]))
                        step(v.memset(nbr, 1.0))
                        step(v.tensor_tensor_scan(rank, nbr, nbr, 0.0, ALU.add, ALU.bypass))
                        n_kept = dve.value_load(sci[0:1, 2:3], min_val=0, max_val=N)
                        done = steps[0]
                        with dve.Fori(0, NP // 8) as j:
                            with dve.If(n_kept > j * 8):
                                restart()
                                step(v.max(top8[:], vals[:, 0:N]))
                                step(v.tensor_copy(ranked[:, bass.ds(j * 8, 8)], top8[:]))
                                step(v.match_replace(vals[:, 0:N], top8[:], vals[:, 0:N], -BIG))
                        restart()
                        for q, (mul, add, shift) in enumerate(((1.0, 3.0, 2), (1.0, 1.0, 1), (3.0, 3.0, 2))):
                            step(v.tensor_scalar(sci[:, 3:4], sc[:, 4:5], mul, add, ALU.mult, ALU.add))
                            step(v.tensor_scalar(sci[:, 4:5], sci[:, 3:4], shift, None, ALU.logical_shift_right))
                            step(v.tensor_scalar(sc[:, 5:6], sci[:, 4:5], 1.0, None, ALU.max))
                            step(v.tensor_tensor(sc[:, 6:7], sc[:, 4:5], sc[:, 5:6], ALU.subtract))
                            step(v.tensor_scalar(sc[:, 7:8], sc[:, 6:7], 1.0, None, ALU.add))
                            step(v.scalar_tensor_tensor(out=nbr, in0=rank, scalar=sc[:, 7:8], in1=ranked,
                                                        op0=ALU.is_equal, op1=ALU.mult))
                            step(v.tensor_reduce(sc[:, 8 + q:9 + q], nbr, AX.X, ALU.add))
                        step(v.tensor_scalar(sc[:, 12:13], sc[:, 8:9], THIRD_HALF, None, ALU.mult))
                        step(v.scalar_tensor_tensor(out=sc[:, 13:14], in0=sc[:, 9:10], scalar=THIRD_HALF,
                                                    in1=sc[:, 12:13], op0=ALU.mult, op1=ALU.add))
                        step(v.scalar_tensor_tensor(out=sc[:, 14:15], in0=sc[:, 10:11], scalar=THIRD_HALF,
                                                    in1=sc[:, 13:14], op0=ALU.mult, op1=ALU.add))
                        v.scalar_tensor_tensor(out=comb_col[:], in0=x_col[:], scalar=0.5, in1=sc[:, 14:15],
                                               op0=ALU.mult, op1=ALU.add).then_inc(s_rc, 1)
                        dve.wait_ge(s_rp, 1)
                        dve.sem_clear(s_rp)
                        step(v.tensor_tensor(sc[:, 16:17], ps_out[:, 0:1], b_col[:], ALU.add))
                        v.tensor_tensor(out_col[:], sc[:, 16:17], x_col[:], ALU.add).then_inc(s_ro, 1)


_INS = ["x", "adj", "L0_gnn_W", "L0_gnn_b"]


def kernel(**inputs):
    import concourse.bacc as bacc
    from concourse.bass_utils import run_bass_kernel_spmd as run

    nc = bacc.Bacc("TRN2", target_bir_lowering=False, num_devices=1)
    arrays, args = {}, []
    for name in _INS:
        a = np.ascontiguousarray(inputs[name])
        arrays[f"in_{name}"] = a
        args.append(nc.dram_tensor(f"in_{name}", a.shape, mybir.dt.from_np(a.dtype), kind="ExternalInput").ap())
    rows, feats = arrays["in_x"].shape
    args.append(nc.dram_tensor("flag_rows", (rows,), I32, kind="Internal").ap())
    args.append(nc.dram_tensor("out_0", (rows, feats), F32, kind="ExternalOutput").ap())
    build(nc, *args)
    r = run(nc, [arrays], core_ids=[0])
    return r.results[0]["out_0"]
```

```python
from contextlib import ExitStack

import concourse.bass as bass
import numpy as np
from concourse import mybir

F32 = mybir.dt.float32
BF16 = mybir.dt.bfloat16
I32 = mybir.dt.int32
U32 = mybir.dt.uint32
ALU = mybir.AluOpType
ACT = mybir.ActivationFunctionType
AX = mybir.AxisListType

P = 128
GT = 6
RING = 6
BANKS = 3
IN_FLIGHT = 3
AHEAD = 3
CHUNK = 3
BITS = 16
TOP = 16
LEVELS = 3
SLOTS = 12
MID = 16
BIG = float(np.finfo(np.float32).max)
NOROW = 8192
THIRD_HALF = float(np.float32(0.5) * np.float32(1.0 / 3.0))
EXPONENT = 0x7F800000


def build(nc, x, adj, W, b, flag_rows, out):
    N, D = x.shape
    assert D == P
    NW = -(-N // BITS)
    assert NW <= 256 and 8 + BITS <= 24
    NP = NW * BITS
    NT = -(-N // P)
    LAST = N - P
    NG = NT // GT
    TT = NT - NG * GT
    assert 2 <= TT <= min(CHUNK, AHEAD) and AHEAD < GT and IN_FLIGHT <= RING
    assert GT % CHUNK == 0 and GT == RING and GT % BANKS == 0 and NG >= 3
    NC = GT // CHUNK
    MH = MID // 16
    MU = 2 * MH
    NF = (LEVELS + 1) * TOP + 3
    SUM = (LEVELS + 1) * TOP

    with ExitStack() as ctx:
        def sb(name, shape, dt):
            return ctx.enter_context(nc.sbuf_tensor(name, shape, dt))

        def psum(name, shape, dt=F32):
            return ctx.enter_context(nc.psum_tensor(name, shape, dt))

        def sem(name):
            return ctx.enter_context(nc.semaphore(name))

        adj_ring = [sb(f"adj{i}", [P, NP], I32) for i in range(RING)]
        sq_ring = sb("sq_ring", [P, RING, NP], BF16)
        x_grp = sb("x_grp", [P, GT, D], F32)
        x_late = [sb(f"x_late{i}", [P, GT, D], F32) for i in range(2)]
        x_tail = sb("x_tail", [P, TT, D], F32)
        w_in = sb("w_in", [P, D], F32)
        wT = sb("wT", [P, D], F32)
        b_row = sb("b_row", [1, D], F32)
        b_col = sb("b_col", [P, 1], F32)
        ident = sb("ident", [P, P], F32)
        half_ident = sb("half_ident", [P, P], F32)
        ident_bf = sb("ident_bf", [P, P], BF16)
        bit_diag = sb("bit_diag", [P, BITS, P], BF16)
        before = sb("before", [P, P], BF16)
        ones_bf = sb("ones_bf", [P, P], BF16)
        ones_f = sb("ones_f", [P, P], F32)
        word_no = sb("word_no", [1, NW], BF16)
        dest_no = sb("dest_no", [P, P], BF16)
        slot_no = sb("slot_no", [P, TOP], F32)
        row_code = sb("row_code", [P, NT, 2], F32)
        counts_here = sb("counts_here", [P, NT], F32)
        pads = sb("pads", [P, 2, D], F32)
        spread = sb("spread", [MID, MH, P], F32)
        own_slot = sb("own_slot", [P, 8], F32)
        mid_pads = sb("mid_pads", [P, D], F32)
        part_i = sb("part_i", [P, 1], I32)
        part_a = sb("part_a", [P, 1], I32)
        part_f = sb("part_f", [P, 2], F32)
        sign_f = sb("sign_f", [P, 1], F32)
        rest_words = sb("rest_words", [P, 2, NW], F32)
        row_sum = sb("row_sum", [P, NT], F32)
        words = sb("words", [P, GT, TOP], I32)
        low_i = sb("low_i", [P, GT, TOP], I32)
        rest = sb("rest", [P, GT, TOP], F32)
        fields = sb("fields", [P, GT, NF], F32)
        present = sb("present", [P, GT, LEVELS * TOP], BF16)
        count = sb("count", [P, GT], F32)
        same = sb("same", [P, GT], F32)
        listed = sb("listed", [P, GT], F32)
        upto10 = sb("upto10", [P, GT], F32)
        slow = sb("slow", [P, NT], F32)
        flags = sb("flags", [P, 3, GT], BF16)
        mid_here = sb("mid_here", [P, 1], F32)
        mid_before = sb("mid_before", [P, 1], BF16)
        place = sb("place", [P, 3, NT], BF16)
        hot = sb("hot", [P, 2, GT, P], BF16)
        hot_mid = sb("hot_mid", [P, GT, MID], BF16)
        hotT = sb("hotT", [P, 2, 2, GT * P], F32)
        exponent = sb("exponent", [P, 2, LEVELS * TOP], I32)
        col_base = sb("col_base", [P, 2, TOP], F32)
        cand = sb("cand", [P, 2, LEVELS * TOP], F32)
        cand_rest = sb("cand_rest", [P, LEVELS * TOP], F32)
        top_a = sb("top_a", [P, 8], F32)
        top_b = sb("top_b", [P, TOP], F32)
        gone = sb("gone", [P, 2], F32)
        odd = sb("odd", [P, 1], F32)
        kept = sb("kept", [P, TOP], F32)
        keys = sb("keys", [P, SLOTS], F32)
        keys0 = sb("keys0", [P, SLOTS], F32)
        missing = sb("missing", [P, SLOTS], F32)
        idx = sb("idx", [P, SLOTS], U32)
        idx_tail = sb("idx_tail", [P, SLOTS], U32)
        w_new = sb("w_new", [P, 2], F32)
        w_low = sb("w_low", [P, 2], F32)
        gathered = sb("gathered", [P, SLOTS, D], F32)
        gathered_tail = sb("gathered_tail", [P, SLOTS, D], F32)
        ga = sb("ga", [P, SLOTS, D], F32)
        gb = sb("gb", [P, SLOTS, D], F32)
        agg = sb("agg", [P, 2, D], F32)
        combT = sb("combT", [P, CHUNK * P], F32)
        res = sb("res", [P, NC, CHUNK, D], F32)
        mid = sb("mid", [MID, NF], F32)
        mid_exp = sb("mid_exp", [MID, LEVELS * TOP], I32)
        mid_base = sb("mid_base", [MID, TOP], F32)
        mid_cand = sb("mid_cand", [MID, LEVELS * TOP], F32)
        mid_crest = sb("mid_crest", [MID, LEVELS * TOP], F32)
        mid_list = sb("mid_list", [MID, TOP], F32)
        mid_gone = sb("mid_gone", [MID, 3], F32)
        mid_kept = sb("mid_kept", [MID, TOP], F32)
        mid_rest = sb("mid_rest", [MID, TOP], F32)
        mid_top = sb("mid_top", [MID, TOP], F32)
        mid_miss = sb("mid_miss", [MID, TOP], F32)
        mid_row = sb("mid_row", [MID, 1], U32)
        mid_ndiag = sb("mid_ndiag", [MID, MID], F32)
        mid_sel = sb("mid_sel", [P, MU, 8], F32)
        mid_idxf = sb("mid_idxf", [P, MU], F32)
        mid_idx = sb("mid_idx", [P, MU], U32)
        mid_x = sb("mid_x", [MID, D], F32)
        mid_g = sb("mid_g", [P, MU, D], F32)
        mid_v = sb("mid_v", [P, MID, TOP], F32)
        mid_below = sb("mid_below", [P, MID, TOP], F32)
        mid_sorted = sb("mid_sorted", [P, MID, TOP], F32)
        mid_part = sb("mid_part", [P, MID, 5], F32)
        mid_w = sb("mid_w", [P, 4, MID], F32)
        mid_t = sb("mid_t", [P, 2, MID], F32)
        mid_out = sb("mid_out", [MID, D], F32)
        slow_i = sb("slow_i", [P, NT], I32)
        slow_sum = sb("slow_sum", [P, 1], F32)
        slow_n = sb("slow_n", [P, 1], I32)
        top8 = sb("top8", [P, 8], F32)
        sc = sb("sc", [P, 24], F32)
        sci = sb("sci", [P, 8], I32)
        x_col = sb("x_col", [P, 1], F32)
        comb_col = sb("comb_col", [P, 1], F32)
        out_col = sb("out_col", [P, 1], F32)
        a_row = adj_ring[0]
        nbr = adj_ring[1][:].bitcast(F32)
        rank = adj_ring[2][:].bitcast(F32)
        vals = adj_ring[3][:].bitcast(F32)
        ranked = adj_ring[4][:].bitcast(F32)
        slow_row = adj_ring[5][0:1, 0:N]
        xT = sq_ring[:].rearrange("p r n -> p (r n)").bitcast(F32)[:, 0:N]

        ps_words = [psum(f"ps_words{i}", [P, 512]) for i in range(BANKS)]
        ps_small = psum("ps_small", [P, 512])
        ps_hotT = psum("ps_hotT", [P, 1024], BF16)
        ps_comb = psum("ps_comb", [P, 512])
        ps_out = [psum(f"ps_out{c}", [P, 512]) for c in range(NC)]
        ps_mT = ps_out[1]
        ps_place = ps_small[:, 0:3 * GT].rearrange("p (c t) -> p c t", c=3)
        ps_bl = ps_small[:, 32:32 + 2 * (SUM + 1)].rearrange("p (c f) -> p c f", c=2)
        ps_mid = ps_small[0:MID, 256:256 + NF]
        high = fields[:].rearrange("p t f -> p (t f)").bitcast(BF16).rearrange(
            "p (t f h) -> p t f h", f=NF, h=2)[:, :, :, 1]

        s_x = sem("x_loaded")
        s_x_late = sem("late_x_loaded")
        s_x_tail = sem("tail_x_loaded")
        s_wb = sem("weights_loaded")
        s_adj = [sem(f"adj_loaded{i}") for i in range(RING)]
        s_loads = sem("loads_released")
        s_pool_step = sem("pool_step")
        s_const = sem("pool_constants_ready")
        s_vconst = sem("vector_constants_ready")
        s_wps = sem("w_transposed")
        s_wT = sem("wT_ready")
        s_sq = sem("adj_squared")
        s_words = sem("words_packed")
        s_top = sem("words_listed")
        s_flags = sem("flags_ready")
        s_place = sem("places_counted")
        s_hot = sem("hot_ready")
        s_comp = sem("blocks_filled")
        s_idx = sem("indices_ready")
        s_pads = sem("pads_written")
        s_go = sem("gathers_issued")
        s_gath = sem("rows_gathered")
        s_gath_tail = sem("tail_rows_gathered")
        s_first = sem("slots_read")
        s_agg = sem("agg_ready")
        s_hps = sem("hotT_in_psum")
        s_hT = sem("hotT_copied")
        s_cps = sem("comb_in_psum")
        s_comb = sem("comb_copied")
        s_ops = sem("out_in_psum")
        s_res = sem("result_ready")
        s_wr = sem("result_written")
        s_wr_tail = sem("tail_written")
        s_step = sem("vector_step")
        s_passed = sem("vector_past_wait")
        s_mpads = sem("mid_pads_written")
        s_mkeys = sem("mid_keys_ready")
        s_mspread = sem("mid_keys_spread")
        s_midx = sem("mid_indices_ready")
        s_mgath = sem("mid_rows_gathered")
        s_mT = sem("mid_transposed")
        s_mS = sem("mid_sorted_layout_ready")
        s_mxT = sem("mid_x_transposed")
        s_mcomb = sem("mid_comb_ready")
        s_mops = sem("mid_out_in_psum")
        s_mres = sem("mid_result_ready")
        s_mwr = sem("mid_written")
        s_slsum = sem("slow_summed")
        s_slps = sem("slow_total_in_psum")
        s_sln = sem("slow_count_ready")
        s_slsc = sem("slow_scratch_written")
        s_slin = sem("slow_inputs_loaded")
        s_ra = sem("slow_row_loaded")
        s_rc = sem("slow_comb_ready")
        s_rp = sem("slow_out_in_psum")
        s_ro = sem("slow_result_ready")
        s_rw = sem("slow_row_written")

        block = ctx.enter_context(nc.Block())

        def groups(eng, front):
            front(0, GT, 0)
            front(1, GT, 1)
            with eng.Fori(2, NG - 1) as g:
                front(g, GT, 2)
            front(NG - 1, GT, 2)
            front(NG, TT, 2)

        @block.sync
        def _(sp):
            def load(g, i, wait):
                if wait:
                    sp.wait_ge(s_sq, g * GT + (i + 1 - RING))
                    sp.sem_inc(s_loads, 1)
                if wait or i >= IN_FLIGHT:
                    sp.wait_ge(s_adj[(i - IN_FLIGHT) % RING], g * 16 + (16 if i >= IN_FLIGHT else 0))
                    sp.sem_inc(s_loads, 1)
                t = g * GT + i
                src = adj[LAST:N, :] if isinstance(g, int) and t == NT - 1 else adj[bass.ds(t * P, P), :]
                sp.dma_start(adj_ring[i % RING][:, 0:N], src).then_inc(s_adj[i % RING], 16)

            def front(g, tiles, older):
                for i in range(tiles):
                    load(g, i, wait=older > 0)
                    if older == 0 and i == 0:
                        sp.dma_start(w_in[:], W).then_inc(s_wb, 16)
                        sp.dma_start(b_row[:], b.rearrange("(a d) -> a d", a=1)).then_inc(s_wb, 16)
                        sp.dma_start(b_col[:], b.rearrange("(d a) -> d a", a=1)).then_inc(s_wb, 16)

            groups(sp, front)

            sp.wait_ge(s_res, NG * NC + 1)
            sp.dma_start(out[NG * GT * P:LAST + 1, :].rearrange("(t p) d -> p t d", p=P),
                         res[:, 0, 0:TT - 1, :]).then_inc(s_wr_tail, 16)
            sp.dma_start(out[LAST + 1:LAST + 113, :], res[1:113, 0, TT - 1, :]).then_inc(s_wr_tail, 16)
            sp.dma_start(out[LAST + 113:N, :], res[113:P, 0, TT - 1, :]).then_inc(s_wr_tail, 16)

            sp.wait_ge(s_sln, 1)
            n_slow = sp.value_load(slow_n[0:1, 0:1], min_val=0, max_val=N)
            with sp.If(n_slow > 0):
                sp.dma_start(flag_rows[0:(NT - 1) * P].rearrange("(t p) -> p t", p=P),
                             slow_i[:, 0:NT - 1], allow_slow_non_contiguous=True).then_inc(s_slsc, 16)
                sp.dma_start(flag_rows[(NT - 1) * P:N].rearrange("(p a) -> p a", a=1),
                             slow_i[NT * P - N:P, NT - 1:NT], allow_slow_non_contiguous=True).then_inc(s_slsc, 16)
                sp.wait_ge(s_mwr, 16)
                sp.wait_ge(s_slsc, 32)
                sp.dma_start(slow_row, flag_rows.rearrange("(a n) -> a n", a=1)).then_inc(s_slin, 16)
                sp.dma_start(xT, x.rearrange("n d -> d n"), allow_slow_non_contiguous=True).then_inc(s_slin, 16)
                sp.wait_ge(s_slin, 32)
                with sp.Fori(0, N) as r:
                    is_slow = sp.value_load(slow_row[0:1, bass.ds(r, 1)], min_val=0, max_val=1)
                    with sp.If(is_slow > 0):
                        sp.dma_start(a_row[:, 0:N], adj[bass.ds(r, 1), :].broadcast_to([P, N])).then_inc(s_ra, 16)
                        sp.wait_ge(s_ro, 1)
                        sp.sem_clear(s_ro)
                        sp.dma_start(out[bass.ds(r, 1), :].rearrange("a d -> d a"), out_col[:],
                                     allow_slow_non_contiguous=True).then_inc(s_rw, 16)
                        sp.wait_ge(s_rw, 16)
                        sp.sem_clear(s_rw)

        @block.gpsimd
        def _(pool):
            steps = [0]

            def step(ins):
                steps[0] += 1
                ins.then_inc(s_pool_step, 1)
                pool.wait_ge(s_pool_step, steps[0])

            step(nc.gpsimd.memset(ident[:], 0.0))
            step(nc.gpsimd.affine_select(out=ident[:], in_=ident[:], compare_op=ALU.not_equal, fill=1.0, base=0,
                                         pattern=[[-1, P]], channel_multiplier=1))
            step(nc.gpsimd.memset(ones_bf[:], 1.0))
            step(nc.gpsimd.affine_select(out=before[:], in_=ones_bf[:], compare_op=ALU.is_gt, fill=0.0, base=0,
                                         pattern=[[1, P]], channel_multiplier=-1))
            step(nc.gpsimd.iota(word_no[:], [[1, NW]], base=0, channel_multiplier=0,
                                allow_small_or_imprecise_dtypes=True))
            nc.gpsimd.memset(ones_f[:], 1.0).then_inc(s_const, 1)
            step(nc.gpsimd.iota(dest_no[:], [[1, P]], base=1, channel_multiplier=0,
                                allow_small_or_imprecise_dtypes=True))
            step(nc.gpsimd.iota(slot_no[:], [[1, TOP]], base=0, channel_multiplier=0,
                                allow_small_or_imprecise_dtypes=True))
            step(nc.gpsimd.iota(row_code[:, :, 0], [[P, NT]], base=-NOROW, channel_multiplier=0,
                                allow_small_or_imprecise_dtypes=True))
            step(nc.gpsimd.iota(row_code[:, NT - 1:NT, 0], [[0, 1]], base=LAST // 64 * 64 - NOROW,
                                channel_multiplier=0, allow_small_or_imprecise_dtypes=True))
            step(nc.gpsimd.iota(row_code[:, :, 1], [[0, NT]], base=0, channel_multiplier=1,
                                allow_small_or_imprecise_dtypes=True))
            step(nc.gpsimd.iota(row_code[:, NT - 1:NT, 1], [[0, 1]], base=LAST % 64, channel_multiplier=1,
                                allow_small_or_imprecise_dtypes=True))
            step(nc.gpsimd.memset(counts_here[:], 1.0))
            step(nc.gpsimd.memset(counts_here[0:NT * P - N, NT - 1:NT], 0.0))
            step(nc.gpsimd.memset(pads[:, 0, :], -BIG))
            step(nc.gpsimd.memset(pads[:, 1, :], BIG))
            for slots in (gathered, gathered_tail):
                step(nc.gpsimd.memset(slots[:], 0.0))
                step(nc.gpsimd.tensor_copy(slots[:, SLOTS - 2:SLOTS, :], pads[:]))
            step(nc.gpsimd.memset(mid_x[:], 0.0))
            step(nc.gpsimd.iota(spread[:], [[16, MH], [1, 16], [0, 8]], base=0, channel_multiplier=-1,
                                allow_small_or_imprecise_dtypes=True))
            nc.gpsimd.iota(part_i[:], [[0, 1]], base=0, channel_multiplier=1).then_inc(s_const, 1)

            def load_x(g):
                if not isinstance(g, int) or g > 0:
                    pool.wait_ge(s_res, g * NC)
                    pool.sem_inc(s_go, 1)
                pool.dma_start(x_grp[:], x[bass.ds(g * (GT * P), GT * P), :].rearrange("(t p) d -> p t d", p=P)
                               ).then_inc(s_x, 16)

            def back(g, tiles):
                for c in range(-(-tiles // CHUNK)):
                    pool.wait_ge(s_res, g * NC + (c + 1))
                    pool.sem_inc(s_go, 1)
                    n = min(CHUNK, tiles - c * CHUNK)
                    rows = out[bass.ds(g * (GT * P) + c * CHUNK * P, n * P), :]
                    pool.dma_start(rows.rearrange("(t p) d -> p t d", p=P), res[:, c, 0:n, :]).then_inc(s_wr, 16)

            def front(g, tiles, older):
                tail = tiles < GT
                slots, indices, landed = (gathered_tail, idx_tail, s_gath_tail) if tail else (gathered, idx, s_gath)
                if older and not tail:
                    pool.wait_ge(s_first, g)
                    pool.sem_inc(s_go, 1)
                    nc.gpsimd.tensor_copy(slots[:, SLOTS - 2:SLOTS, :], pads[:]).then_inc(s_pads, 1)
                    pool.wait_ge(s_pads, g)
                pool.wait_ge(s_idx, g + 1)
                pool.sem_inc(s_go, 1)
                for s in range(SLOTS):
                    nc.gpsimd.indirect_dma_start(
                        slots[:, s, :], None, x,
                        bass.IndirectOffsetOnAxis(ap=indices[:, s:s + 1], axis=0),
                        bounds_check=N - 1, oob_is_err=False).then_inc(landed, 16)
                if older == 0:
                    load_x(0)
                if older == 1:
                    pool.dma_start(x_tail[:, 0:TT - 1, :],
                                   x[NG * GT * P:(NT - 1) * P, :].rearrange("(t p) d -> p t d", p=P)).then_inc(s_x_tail, 16)
                    pool.dma_start(x_tail[:, TT - 1, :], x[LAST:N, :]).then_inc(s_x_tail, 16)
                    for i in range(2):
                        first = (NG - 2 + i) * GT * P
                        pool.dma_start(x_late[i][:], x[first:first + GT * P, :].rearrange("(t p) d -> p t d", p=P)
                                       ).then_inc(s_x_late, 16)
                if older == 2:
                    if not isinstance(g, int) or g < NG - 1:
                        load_x(g - 1)
                    back(g - 2, GT)

            groups(pool, front)
            pool.wait_ge(s_midx, 1)
            nc.gpsimd.indirect_dma_start(mid_x[:], None, x, bass.IndirectOffsetOnAxis(ap=mid_row[:], axis=0),
                                         bounds_check=N - 1, oob_is_err=False).then_inc(s_mgath, 16)
            pool.wait_ge(s_midx, 2)
            pool.wait_ge(s_mpads, 1)
            for u in range(MU):
                nc.gpsimd.indirect_dma_start(mid_g[:, u, :], None, x,
                                             bass.IndirectOffsetOnAxis(ap=mid_idx[:, u:u + 1], axis=0),
                                             bounds_check=N - 1, oob_is_err=False).then_inc(s_mgath, 16)
            back(NG - 1, GT)
            pool.wait_ge(s_mres, 1)
            pool.wait_ge(s_wr, 16 * NG * NC)
            pool.wait_ge(s_wr_tail, 48)
            nc.gpsimd.indirect_dma_start(out, bass.IndirectOffsetOnAxis(ap=mid_row[:], axis=0), mid_out[:], None,
                                         bounds_check=N - 1, oob_is_err=False).then_inc(s_mwr, 16)
            pool.wait_ge(s_mwr, 16)

        @block.scalar
        def _(act):
            def square(g, i, wait):
                act.wait_ge(s_adj[i % RING], g * 16 + 16)
                if wait:
                    act.wait_ge(s_words, g * GT + (i + 1 - RING))
                else:
                    act.wait_ge(s_vconst, 1)
                nc.scalar.activation(sq_ring[:, i % RING, :], adj_ring[i % RING][:], ACT.Square,
                                     accum_out=row_sum[:, bass.ds(g * GT + i, 1)]).then_inc(s_sq, 1)

            def hot_copy(g, tiles, k):
                act.wait_ge(s_hps, g * 2 + (k + 1))
                if not isinstance(g, int) or g >= 2:
                    act.wait_ge(s_cps, g * NC - NC)
                nc.scalar.activation(hotT[:, bass.ds(g % 2, 1), k, 0:tiles * P].rearrange("p o n -> p (o n)"),
                                     ps_hotT[:, 0:tiles * P], ACT.Copy).then_inc(s_hT, 1)

            def comb_copy(g, tiles, c):
                n = min(CHUNK, tiles - c * CHUNK) * P
                act.wait_ge(s_cps, g * NC + (c + 1))
                if not (isinstance(g, int) and g == 0 and c == 0):
                    act.wait_ge(s_ops, g * NC + c)
                nc.scalar.activation(combT[:, 0:n], ps_comb[:, 0:n], ACT.Copy).then_inc(s_comb, 1)

            def result_copy(g, tiles, c):
                n = min(CHUNK, tiles - c * CHUNK)
                act.wait_ge(s_ops, g * NC + (c + 1))
                if not isinstance(g, int) or g > 0:
                    act.wait_ge(s_wr, g * (NC * 16))
                nc.scalar.activation(res[:, c, 0:n, :], ps_out[c][:, 0:n * P].rearrange("p (t d) -> p t d", d=D),
                                     ACT.Copy).then_inc(s_res, 1)

            def front(g, tiles, older):
                if older:
                    hot_copy(g - 1, GT, 0)
                    if tiles < GT:
                        hot_copy(g - 1, GT, 1)
                for i in range(0 if older == 0 else AHEAD, tiles):
                    square(g, i, wait=older > 0)
                    if older and i == AHEAD:
                        hot_copy(g - 1, GT, 1)
                    if older == 0 and i == 0:
                        act.wait_ge(s_wps, 1)
                        nc.scalar.activation(wT[:], ps_comb[:, 0:D], ACT.Copy).then_inc(s_wT, 1)
                if tiles == GT:
                    for i in range(TT if isinstance(g, int) and g == NG - 1 else AHEAD):
                        square(g + 1, i, wait=True)
                if older == 2:
                    comb_copy(g - 2, GT, 0)
                    result_copy(g - 2, GT, 0)
                    comb_copy(g - 2, GT, 1)
                    result_copy(g - 2, GT, 1)

            groups(act, front)
            for u in range(MU):
                last = nc.scalar.activation(mid_g[:, u, :], mid_pads[:], ACT.Copy)
            last.then_inc(s_mpads, 1)
            hot_copy(NG, TT, 0)
            hot_copy(NG, TT, 1)
            comb_copy(NG - 1, GT, 0)
            result_copy(NG - 1, GT, 0)
            comb_copy(NG - 1, GT, 1)
            result_copy(NG - 1, GT, 1)
            act.wait_ge(s_mT, 1)
            for u in range(MU):
                h, sh = u // 2, u % 2
                last = nc.scalar.activation(mid_v[:, h * 16:h * 16 + 16, sh * 8:sh * 8 + 8],
                                            ps_mT[:, u * P:(u + 1) * P].rearrange("p (b s) -> p b s", s=8), ACT.Copy)
            last.then_inc(s_mS, 1)
            comb_copy(NG, TT, 0)
            result_copy(NG, TT, 0)

        @block.tensor
        def _(pe):
            pe.wait_ge(s_const, 1)
            pe.wait_ge(s_wb, 48)
            nc.tensor.transpose(ps_comb[:, 0:D], w_in[:], ident[:]).then_inc(s_wps, 1)
            pe.wait_ge(s_vconst, 1)

            def pack(g, i, wait):
                pe.wait_ge(s_sq, g * GT + (i + 1))
                if wait:
                    pe.wait_ge(s_top, g * GT + (i + 1 - BANKS))
                bank = ps_words[i % BANKS][:, 0:NW]
                nc.tensor.matmul(bank, ones_bf[0:1, :], word_no[0:1, :], start=True, stop=False)
                for k in range(BITS):
                    last = nc.tensor.matmul(bank, bit_diag[:, k, :], sq_ring[:, i % RING, k * NW:(k + 1) * NW],
                                            start=False, stop=(k == BITS - 1))
                last.then_inc(s_words, 1)

            def turn_hot(g, tiles, k):
                pe.wait_ge(s_hot, g + 1)
                if not (isinstance(g, int) and g == 0 and k == 0):
                    pe.wait_ge(s_hT, g * 2 + k)
                for i in range(tiles):
                    last = nc.tensor.transpose(ps_hotT[:, i * P:(i + 1) * P], hot[:, k, i, :], ident_bf[:])
                last.then_inc(s_hps, 1)

            def x_of(g):
                return {NG - 2: x_late[0], NG - 1: x_late[1], NG: x_tail}.get(g, x_grp) if isinstance(g, int) else x_grp

            def combine(g, tiles, c):
                n = min(CHUNK, tiles - c * CHUNK)
                xs = x_of(g)
                pe.wait_ge(s_agg, g + 1)
                pe.wait_ge(s_hT, g * 2 + 2)
                if xs is x_tail:
                    pe.wait_ge(s_x_tail, 32)
                elif xs is not x_grp:
                    pe.wait_ge(s_x_late, 32)
                else:
                    pe.wait_ge(s_x, g * 16 + 16)
                if isinstance(g, int) and g == 0 and c == 0:
                    pe.wait_ge(s_wT, 1)
                else:
                    pe.wait_ge(s_comb, g * NC + c)
                for k in range(2):
                    part = hotT[:, bass.ds(g % 2, 1), k, c * CHUNK * P:(c * CHUNK + n) * P]
                    nc.tensor.matmul(ps_comb[:, 0:n * P], agg[:, k, :], part.rearrange("p o n -> p (o n)"),
                                     start=(k == 0), stop=False)
                for i in range(n):
                    last = nc.tensor.matmul(ps_comb[:, i * P:(i + 1) * P], xs[:, c * CHUNK + i, :],
                                            half_ident[:], start=False, stop=(i == n - 1))
                last.then_inc(s_cps, 1)

            def project(g, tiles, c):
                n = min(CHUNK, tiles - c * CHUNK)
                xs = x_of(g)
                if not isinstance(g, int) or g > 0:
                    pe.wait_ge(s_res, g * NC)
                nc.tensor.matmul(ps_out[c][:, 0:n * P], ident[:], xs[:, c * CHUNK:c * CHUNK + n, :].rearrange(
                    "p t d -> p (t d)"), start=True, stop=False)
                pe.wait_ge(s_comb, g * NC + (c + 1))
                for i in range(n):
                    nc.tensor.matmul(ps_out[c][:, i * P:(i + 1) * P], ones_f[0:1, :], b_row[:],
                                     start=False, stop=False)
                    last = nc.tensor.matmul(ps_out[c][:, i * P:(i + 1) * P], combT[:, i * P:(i + 1) * P], wT[:],
                                            start=False, stop=(i == n - 1))
                last.then_inc(s_ops, 1)

            def places(g, tiles):
                pe.wait_ge(s_flags, g + 1)
                nc.tensor.matmul(ps_place[:, :, 0:tiles], before[:], flags[:, :, 0:tiles], start=True, stop=False)
                for d in range(1, tiles):
                    nc.tensor.matmul(ps_place[:, :, d:tiles], ones_bf[:], flags[:, :, 0:tiles - d],
                                     start=False, stop=False)
                for i in range(tiles):
                    last = nc.tensor.matmul(ps_place[:, 2, i:i + 1], ones_bf[:], mid_before[:], start=False,
                                            stop=(i == tiles - 1))
                last.then_inc(s_place, 1)

            def fill_blocks(g, tiles):
                pe.wait_ge(s_hot, g + 1)
                for k in range(2):
                    for i in range(tiles):
                        nc.tensor.matmul(ps_bl[:, k, :], hot[:, k, i, :], high[:, i, 0:SUM + 1],
                                         start=(i == 0), stop=(i == tiles - 1))
                for i in range(tiles):
                    last = nc.tensor.matmul(ps_mid, hot_mid[:, i, :], high[:, i, :], start=(i == 0),
                                            stop=(i == tiles - 1))
                last.then_inc(s_comp, 1)

            def front(g, tiles, older):
                if older:
                    turn_hot(g - 1, GT, 0)
                    if tiles < GT:
                        turn_hot(g - 1, GT, 1)
                for i in range(0 if older == 0 else TT, tiles):
                    pack(g, i, wait=older > 0 or i >= BANKS)
                    if older and i == TT:
                        turn_hot(g - 1, GT, 1)
                places(g, tiles)
                if tiles == GT:
                    pack(g + 1, 0, wait=True)
                fill_blocks(g, tiles)
                if tiles == GT:
                    for i in range(1, TT):
                        pack(g + 1, i, wait=True)
                if older == 2:
                    combine(g - 2, GT, 0)
                    project(g - 2, GT, 0)
                    combine(g - 2, GT, 1)
                    project(g - 2, GT, 1)

            groups(pe, front)
            turn_hot(NG, TT, 0)
            turn_hot(NG, TT, 1)
            pe.wait_ge(s_mkeys, 1)
            for h in range(MH):
                nc.tensor.matmul(ps_words[0][:, h * TOP:(h + 1) * TOP], spread[:, h, :], mid_top[:],
                                 start=True, stop=True)
            nc.tensor.matmul(ps_words[0][:, 64:64 + MID], ones_f[0:MID, :], mid_ndiag[:], start=True,
                             stop=True).then_inc(s_mspread, 1)
            combine(NG - 1, GT, 0)
            project(NG - 1, GT, 0)
            combine(NG - 1, GT, 1)
            project(NG - 1, GT, 1)
            pe.wait_ge(s_mgath, 16 * (MU + 1))
            pe.wait_ge(s_res, NG * NC)
            for u in range(MU):
                last = nc.tensor.transpose(ps_mT[:, u * P:(u + 1) * P], mid_g[:, u, :], ident[:])
            last.then_inc(s_mT, 1)
            nc.tensor.matmul(ps_words[1][:, 0:MID], mid_x[:], half_ident[0:MID, 0:MID], start=True,
                             stop=True).then_inc(s_mxT, 1)
            combine(NG, TT, 0)
            project(NG, TT, 0)
            pe.wait_ge(s_mcomb, 1)
            nc.tensor.matmul(ps_words[2][0:MID, 0:D], mid_t[:, 1, :], wT[:], start=True, stop=False)
            nc.tensor.matmul(ps_words[2][0:MID, 0:D], ones_f[0:1, 0:MID], b_row[:], start=False,
                             stop=True).then_inc(s_mops, 1)
            pe.wait_ge(s_slsum, 1)
            nc.tensor.matmul(ps_small[:, 0:1], ones_f[:], slow_sum[:], start=True, stop=True).then_inc(s_slps, 1)
            pe.wait_ge(s_sln, 1)
            n_slow = pe.value_load(slow_n[0:1, 0:1], min_val=0, max_val=N)
            with pe.If(n_slow > 0):
                pe.wait_ge(s_slin, 32)
                with pe.Fori(0, N) as r:
                    is_slow = pe.value_load(slow_row[0:1, bass.ds(r, 1)], min_val=0, max_val=1)
                    with pe.If(is_slow > 0):
                        pe.wait_ge(s_rc, 1)
                        pe.sem_clear(s_rc)
                        nc.tensor.matmul(ps_out[0][:, 0:1], wT[:], comb_col[:], start=True, stop=True).then_inc(s_rp, 1)

        @block.vector
        def _(dve):
            v = nc.vector
            steps = [0]

            def step(ins):
                steps[0] += 1
                ins.then_inc(s_step, 1)
                dve.wait_ge(s_step, steps[0])

            def restart():
                dve.sem_clear(s_step)
                steps[0] = 0

            def did(ins):
                steps[0] += 1
                ins.then_inc(s_step, 1)
                return steps[0]

            def need(n):
                dve.wait_ge(s_step, n)

            for i in range(RING):
                step(v.memset(adj_ring[i][:, N:NP], 0))
            step(v.memset(mid[:], 0.0))
            step(v.memset(mid_before[:], 0.0))
            step(v.memset(slow[:], 0.0))
            step(v.memset(fields[:], 0.0))
            step(v.memset(w_new[:], 0.0))
            dve.wait_ge(s_const, 1)
            step(v.tensor_copy(ident_bf[:], ident[:]))
            step(v.tensor_scalar(half_ident[:], ident[:], 0.5, None, ALU.mult))
            for k in range(BITS):
                last = v.tensor_scalar(bit_diag[:, k, :], ident_bf[:], float(2 ** (k + 8)), None, ALU.mult)
            last.then_inc(s_vconst, 1)
            dve.wait_ge(s_const, 2)
            step(v.tensor_scalar(spread[:], spread[:], 0.0, None, ALU.is_equal))
            step(v.tensor_scalar(part_a[:], part_i[:], 7, None, ALU.bitwise_and))
            step(v.tensor_copy(part_f[:, 0:1], part_a[:]))
            step(v.tensor_scalar(part_a[:], part_i[:], 1, None, ALU.bitwise_and))
            step(v.tensor_copy(part_f[:, 1:2], part_a[:]))
            step(v.tensor_scalar(own_slot[:], slot_no[:, 0:8], part_f[:, 0:1], None, ALU.is_equal))
            step(v.tensor_scalar(sign_f[:], part_f[:, 1:2], 2.0, -1.0, ALU.mult, ALU.add))
            step(v.tensor_scalar(mid_pads[:], pads[:, 1, :], sign_f[:, 0:1], None, ALU.mult))

            def list_words(g, tiles):
                banks = [ps_words[i % BANKS][:, 0:NW] for i in tiles]
                dve.wait_ge(s_words, g * GT + (tiles[-1] + 1))
                dve.sem_inc(s_passed, 1)
                high8 = [did(v.max(words[:, i, 0:8], bank)) for i, bank in zip(tiles, banks)]
                less8 = []
                for k, i in enumerate(tiles):
                    need(high8[k])
                    less8.append(did(v.match_replace(rest_words[:, k, :], words[:, i, 0:8], banks[k], -1.0)))
                for k, i in enumerate(tiles):
                    need(less8[k])
                    v.max(words[:, i, 8:16], rest_words[:, k, :]).then_inc(s_top, 1)

            def decode(g, tiles):
                w, lo, rs = words[:, 0:tiles, :], low_i[:, 0:tiles, :], rest[:, 0:tiles, :]
                level = [fields[:, 0:tiles, l * TOP:(l + 1) * TOP] for l in range(LEVELS)]
                total = fields[:, 0:tiles, SUM]
                here = counts_here[:, bass.ds(g * GT, tiles)]
                dve.wait_ge(s_top, g * GT + tiles)
                step(v.tensor_scalar(lo, w, 255, None, ALU.bitwise_and))
                step(v.tensor_tensor(rs, w, lo, ALU.subtract))
                did(v.tensor_copy(fields[:, 0:tiles, LEVELS * TOP:SUM], lo))
                for l in range(LEVELS):
                    top = did(v.tensor_scalar(level[l].bitcast(I32), rs.bitcast(I32), EXPONENT, None,
                                              ALU.bitwise_and))
                    if l == 0:
                        did(v.tensor_tensor(total, row_sum[:, bass.ds(g * GT, tiles)], here, ALU.mult))
                    if l == 1:
                        did(v.tensor_copy(fields[:, 0:tiles, SUM + 1:SUM + 3], row_code[:, bass.ds(g * GT, tiles), :]))
                    need(top)
                    if l < LEVELS - 1:
                        step(v.tensor_tensor(rs, rs, level[l], ALU.subtract))
                step(v.tensor_scalar(present[:, 0:tiles, :], fields[:, 0:tiles, 0:LEVELS * TOP], 0.0, None, ALU.is_gt))
                n = count[:, 0:tiles]
                step(v.tensor_reduce(n, present[:, 0:tiles, :], AX.X, ALU.add))
                sm, li, up = same[:, 0:tiles], listed[:, 0:tiles], upto10[:, 0:tiles]
                step(v.tensor_tensor(sm, n, total, ALU.is_equal))
                step(v.scalar_tensor_tensor(out=li, in0=n, scalar=15.0, in1=sm, op0=ALU.is_le, op1=ALU.mult))
                step(v.scalar_tensor_tensor(out=li, in0=n, scalar=6.0, in1=li, op0=ALU.is_ge, op1=ALU.mult))
                did(v.scalar_tensor_tensor(out=slow[:, bass.ds(g * GT, tiles)], in0=total, scalar=6.0, in1=li,
                                           op0=ALU.is_ge, op1=ALU.subtract))
                did(v.scalar_tensor_tensor(out=flags[:, 0, 0:tiles], in0=n, scalar=6.0, in1=li,
                                           op0=ALU.is_le, op1=ALU.mult))
                step(v.scalar_tensor_tensor(out=up, in0=n, scalar=10.0, in1=li, op0=ALU.is_le, op1=ALU.mult))
                did(v.tensor_tensor(flags[:, 1, 0:tiles], up, flags[:, 0, 0:tiles], ALU.subtract))
                v.tensor_tensor(flags[:, 2, 0:tiles], li, up, ALU.subtract).then_inc(s_flags, 1)

            def assign(g, tiles):
                dve.wait_ge(s_place, g + 1)
                pl = place[:, :, bass.ds(g * GT, tiles)]
                step(v.scalar_tensor_tensor(out=pl, in0=ps_place[:, :, 0:tiles], scalar=1.0,
                                            in1=flags[:, :, 0:tiles], op0=ALU.add, op1=ALU.mult))
                if not isinstance(g, int) or g > 0:
                    dve.wait_ge(s_hps, g * 2)
                for k in range(2):
                    v.tensor_tensor(hot[:, k, 0:tiles, :], dest_no[:].unsqueeze(1).broadcast_to([P, tiles, P]),
                                    place[:, k, bass.ds(g * GT, tiles)].unsqueeze(2).broadcast_to([P, tiles, P]),
                                    ALU.is_equal)
                v.tensor_tensor(hot_mid[:, 0:tiles, :], dest_no[:, 0:MID].unsqueeze(1).broadcast_to([P, tiles, MID]),
                                place[:, 2, bass.ds(g * GT, tiles)].unsqueeze(2).broadcast_to([P, tiles, MID]),
                                ALU.is_equal).then_inc(s_hot, 1)
                step(v.tensor_reduce(mid_here[:], flags[:, 2, 0:tiles], AX.X, ALU.add))
                step(v.tensor_tensor(mid_before[:], mid_before[:], mid_here[:], ALU.add))

            def word_base(base, number):
                return did(v.tensor_scalar(base, number, float(1 - NW * (127 + 8)), None, ALU.add))

            def columns(cd, ex, base):
                return did(v.scalar_tensor_tensor(
                    out=cd.rearrange("p (l t) -> p l t", t=TOP), in0=ex.rearrange("p (l t) -> p l t", t=TOP),
                    scalar=float(NW), in1=base.unsqueeze(1).broadcast_to([base.shape[0], LEVELS, TOP]),
                    op0=ALU.mult, op1=ALU.add))

            def block_indices(g, tail):
                dve.wait_ge(s_comp, g + 1)
                out_idx = idx_tail if tail else idx
                wl = w_new
                n = ps_bl[:, 1, SUM:SUM + 1]
                old = did(v.tensor_copy(w_low[:], w_new[:]))
                did(v.tensor_scalar(exponent[:], ps_bl[:, :, 0:LEVELS * TOP].bitcast(I32), 23, None,
                                    ALU.logical_shift_right))
                based = word_base(col_base[:], ps_bl[:, :, LEVELS * TOP:SUM])
                did(v.tensor_tensor(mid[:], mid[:], ps_mid, ALU.add))
                need(based)
                one = columns(cand[:, 1, :], exponent[:, 1, :], col_base[:, 1, :])
                both = columns(cand[:, 0, :], exponent[:, 0, :], col_base[:, 0, :])
                need(one)
                b8 = did(v.max(top_b[:, 0:8], cand[:, 1, :]))
                g0 = did(v.tensor_scalar(gone[:, 0:1], n, 8.0, 3.0, ALU.is_ge, ALU.add))
                need(b8)
                b_rest = did(v.match_replace(cand_rest[:], top_b[:, 0:8], cand[:, 1, :], -1e6))
                need(g0)
                g1 = did(v.scalar_tensor_tensor(out=gone[:, 1:2], in0=n, scalar=10.0, in1=gone[:, 0:1], op0=ALU.is_ge,
                                                op1=ALU.add))
                need(b_rest)
                b16 = did(v.max(top_b[:, 8:16], cand_rest[:]))
                need(both)
                a8 = did(v.max(top_a[:], cand[:, 0, :]))
                need(max(b16, g1))
                kp = did(v.scalar_tensor_tensor(out=kept[:], in0=slot_no[:], scalar=gone[:, 1:2], in1=top_b[:],
                                                op0=ALU.not_equal, op1=ALU.mult))
                od = did(v.scalar_tensor_tensor(out=odd[:], in0=gone[:, 1:2], scalar=-2.0, in1=n, op0=ALU.mult,
                                                op1=ALU.add))
                need(a8)
                ky = did(v.tensor_copy(keys[:, 0:4].rearrange("p (a c) -> p a c", a=2),
                                  top_a[:, 1:7].rearrange("p (a c) -> p a c", a=2)[:, :, 0:2]))
                need(max(kp, od))
                k0 = did(v.tensor_scalar(kept[:, 0:1], kept[:, 0:1], odd[:, 0:1], None, ALU.mult))
                did(v.tensor_scalar(wl[:, 0:1], n, 9.0, THIRD_HALF, ALU.is_ge, ALU.mult))
                need(k0)
                k8 = did(v.max(keys[:, 4:12], kept[:]))
                did(v.tensor_scalar(wl[:, 1:2], n, 9.0, THIRD_HALF, ALU.is_lt, ALU.mult))
                need(k8)
                step(v.tensor_scalar(keys0[:], keys[:], 0.0, -1.0, ALU.max, ALU.add))
                step(v.tensor_scalar(missing[:], keys[:], 0.0, float(NOROW + 1), ALU.is_le, ALU.mult))
                if not tail and (not isinstance(g, int) or g > 0):
                    dve.wait_ge(s_gath, g * (SLOTS * 16))
                v.tensor_tensor(out_idx[:], keys0[:], missing[:], ALU.add).then_inc(s_idx, 1)

            def low_high(dst_lo, dst_hi, a, c):
                if dst_lo is not None:
                    did(v.tensor_tensor(dst_lo, a, c, ALU.min))
                if dst_hi is not None:
                    did(v.tensor_tensor(dst_hi, a, c, ALU.max))

            def layer_done():
                dve.wait_ge(s_step, steps[0])

            def first_layer(g, tail):
                if tail:
                    dve.wait_ge(s_gath_tail, SLOTS * 16)
                else:
                    dve.wait_ge(s_gath, g * (SLOTS * 16) + SLOTS * 16)
                pa = (gathered_tail if tail else gathered)[:].rearrange("p (a c) d -> p a c d", c=2)
                pb = gb[:].rearrange("p (a c) d -> p a c d", c=2)
                did(v.tensor_tensor(pb[:, :, 0, :], pa[:, :, 0, :], pa[:, :, 1, :], ALU.min))
                step(v.tensor_tensor(pb[:, :, 1, :], pa[:, :, 0, :], pa[:, :, 1, :], ALU.max))
                dve.sem_inc(s_first, 1)

            def sort_and_pool(g, wl):
                low_high(ga[:, 3, :], None, gb[:, 1, :], gb[:, 3, :])
                qa = ga[:, 4:12, :].rearrange("p (q h c) d -> p q h (c d)", q=2, h=2)
                qb = gb[:, 4:12, :].rearrange("p (q h c) d -> p q h (c d)", q=2, h=2)
                low_high(qa[:, :, 0, :], qa[:, :, 1, :], qb[:, :, 0, :], qb[:, :, 1, :])
                layer_done()
                la = ga[:, 4:12, :].rearrange("p (q l) d -> p q l d", q=2)
                lb = gb[:, 4:12, :].rearrange("p (q l) d -> p q l d", q=2)
                low_high(lb[:, :, 1, :], lb[:, :, 2, :], la[:, :, 1, :], la[:, :, 2, :])
                layer_done()
                A, B = ga[:, 4:12, :], gb[:, 4:12, :]
                low_high(None, B[:, 4, :], A[:, 0, :], A[:, 4, :])
                low_high(B[:, 3, :], None, A[:, 3, :], A[:, 7, :])
                low_high(A[:, 1:3, :], A[:, 5:7, :], B[:, 1:3, :], B[:, 5:7, :])
                layer_done()
                low_high(B[:, 2, :], A[:, 4, :], A[:, 2, :], B[:, 4, :])
                low_high(A[:, 3, :], B[:, 5, :], B[:, 3, :], A[:, 5, :])
                layer_done()
                low_high(B[:, 1, :], A[:, 2, :], A[:, 1, :], B[:, 2, :])
                low_high(B[:, 3, :], None, A[:, 3, :], A[:, 4, :])
                low_high(A[:, 5, :], None, B[:, 5, :], A[:, 6, :])
                layer_done()
                if not isinstance(g, int) or g > 0:
                    dve.wait_ge(s_cps, g * NC)
                a0, a1 = agg[:, 0, :], agg[:, 1, :]
                w = THIRD_HALF
                z1 = did(v.tensor_scalar(a0, gb[:, 0, :], w, None, ALU.mult))
                o1 = did(v.tensor_scalar(a1, B[:, 1, :], wl[:, 0:1], None, ALU.mult))
                need(z1)
                z2 = did(v.scalar_tensor_tensor(out=a0, in0=gb[:, 2, :], scalar=w, in1=a0, op0=ALU.mult, op1=ALU.add))
                need(o1)
                o2 = did(v.scalar_tensor_tensor(out=a1, in0=A[:, 2, :], scalar=wl[:, 1:2], in1=a1,
                                                op0=ALU.mult, op1=ALU.add))
                need(z2)
                did(v.scalar_tensor_tensor(out=a0, in0=ga[:, 3, :], scalar=w, in1=a0, op0=ALU.mult, op1=ALU.add))
                need(o2)
                step(v.scalar_tensor_tensor(out=a1, in0=B[:, 3, :], scalar=w, in1=a1, op0=ALU.mult, op1=ALU.add))
                v.scalar_tensor_tensor(out=a1, in0=A[:, 5, :], scalar=w, in1=a1, op0=ALU.mult,
                                       op1=ALU.add).then_inc(s_agg, 1)

            def front(g, tiles, older):
                restart()
                if older:
                    list_words(g, (0, 1))
                for i in range(2 if older else 0, tiles):
                    list_words(g, (i,))
                decode(g, tiles)
                assign(g, tiles)
                if older and tiles == GT:
                    first_layer(g - 1, False)
                block_indices(g, tiles < GT)
                if older and tiles == GT:
                    sort_and_pool(g - 1, w_low)

            groups(dve, front)

            first_layer(NG - 1, False)
            sort_and_pool(NG - 1, w_low)

            n = mid[:, SUM:SUM + 1]

            def beyond(k, rows):
                return did(v.scalar_tensor_tensor(out=slow[:], in0=place[:, k, :], scalar=float(rows), in1=slow[:],
                                                  op0=ALU.is_gt, op1=ALU.max))

            did(v.tensor_scalar(mid_exp[:], mid[:, 0:LEVELS * TOP].bitcast(I32), 23, None, ALU.logical_shift_right))
            based = word_base(mid_base[:], mid[:, LEVELS * TOP:SUM])
            g0 = did(v.tensor_scalar(mid_gone[:, 0:1], n, 12.0, 5.0, ALU.is_ge, ALU.add))
            need(based)
            listed_all = columns(mid_cand[:], mid_exp[:], mid_base[:])
            b0 = beyond(0, P)
            need(listed_all)
            first8 = did(v.max(mid_list[:, 0:8], mid_cand[:]))
            need(max(g0, b0))
            g1 = did(v.scalar_tensor_tensor(out=mid_gone[:, 1:2], in0=n, scalar=14.0, in1=mid_gone[:, 0:1],
                                            op0=ALU.is_ge, op1=ALU.add))
            need(first8)
            others = did(v.match_replace(mid_crest[:], mid_list[:, 0:8], mid_cand[:], -1e6))
            b1 = beyond(1, P)
            need(others)
            next8 = did(v.max(mid_list[:, 8:16], mid_crest[:]))
            g2 = did(v.scalar_tensor_tensor(out=mid_gone[:, 2:3], in0=mid_gone[:, 1:2], scalar=-2.0, in1=n,
                                            op0=ALU.mult, op1=ALU.add))
            need(next8)
            kept_all = did(v.scalar_tensor_tensor(out=mid_kept[:], in0=slot_no[0:MID, :], scalar=mid_gone[:, 1:2],
                                                  in1=mid_list[:], op0=ALU.not_equal, op1=ALU.mult))
            b2 = beyond(2, MID)
            need(max(kept_all, g2))
            no0 = did(v.tensor_scalar(mid_kept[:, 0:1], mid_kept[:, 0:1], mid_gone[:, 2:3], None, ALU.mult))
            did(v.scalar_tensor_tensor(out=mid_row[:], in0=mid[:, SUM + 1:SUM + 2], scalar=float(NOROW),
                                       in1=mid[:, SUM + 2:SUM + 3], op0=ALU.add, op1=ALU.add))
            need(no0)
            first8 = did(v.max(mid_top[:, 0:8], mid_kept[:]))
            did(v.tensor_scalar(mid_ndiag[:], ident[0:MID, 0:MID], mid[:, SUM:SUM + 1], None, ALU.mult))
            need(first8)
            step(v.match_replace(mid_rest[:], mid_top[:, 0:8], mid_kept[:], -1e6))
            step(v.max(mid_top[:, 8:16], mid_rest[:]))
            step(v.tensor_scalar(mid_miss[:], mid_top[:], 0.0, float(NOROW + 1), ALU.is_le, ALU.mult))
            step(v.tensor_scalar(mid_top[:], mid_top[:], 0.0, -1.0, ALU.max, ALU.add))
            step(v.tensor_tensor(mid_top[:], mid_top[:], mid_miss[:], ALU.add))
            v.tensor_reduce(slow_sum[:], slow[:], AX.X, ALU.add).then_inc(s_slsum, 1)
            v.tensor_scalar(slow_i[:], slow[:], 0.0, None, ALU.add).then_inc(s_mkeys, 1)
            dve.wait_ge(s_mkeys, 1)
            dve.sem_inc(s_midx, 1)
            dve.wait_ge(s_mspread, 1)
            spread_keys = ps_words[0][:, 0:MH * TOP].rearrange("p (u c) -> p u c", c=8)
            for u in range(MU):
                last = v.tensor_tensor(mid_sel[:, u, :], spread_keys[:, u, :], own_slot[:], ALU.mult)
            step(last)
            step(v.tensor_reduce(mid_idxf[:], mid_sel[:], AX.X, ALU.add))
            v.tensor_copy(mid_idx[:], mid_idxf[:]).then_inc(s_midx, 1)
            n_all = ps_words[0][:, 64:64 + MID]
            for q, (edge, op) in enumerate(((13.0, ALU.is_ge), (13.0, ALU.is_lt), (15.0, ALU.is_lt), (15.0, ALU.is_ge))):
                step(v.tensor_scalar(mid_w[:, q, :], n_all, edge, THIRD_HALF, op, ALU.mult))

            first_layer(NG, True)
            sort_and_pool(NG, w_new)

            dve.wait_ge(s_mS, 1)
            for m in range(MID):
                did(v.max(mid_sorted[:, m, 0:8], mid_v[:, m, :]))
            layer_done()
            for m in range(MID):
                did(v.match_replace(mid_below[:, m, :], mid_sorted[:, m, 0:8], mid_v[:, m, :], -BIG))
            layer_done()
            for m in range(MID):
                did(v.max(mid_sorted[:, m, 8:16], mid_below[:, m, :]))
            layer_done()
            for q, (rank_, weight) in enumerate(((4, 0), (5, 1), (7, None), (10, 2), (11, 3))):
                one = mid_sorted[:, :, TOP - 1 - rank_]
                if weight is None:
                    did(v.tensor_scalar(mid_part[:, :, q], one, THIRD_HALF, None, ALU.mult))
                else:
                    did(v.tensor_tensor(mid_part[:, :, q], one, mid_w[:, weight, :], ALU.mult))
            layer_done()
            t0, t1 = mid_t[:, 0, :], mid_t[:, 1, :]
            step(v.tensor_reduce(t0, mid_part[:], AX.X, ALU.add))
            dve.wait_ge(s_mxT, 1)
            v.tensor_tensor(t1, t0, ps_words[1][:, 0:MID], ALU.add).then_inc(s_mcomb, 1)

            dve.wait_ge(s_mops, 1)
            v.tensor_tensor(mid_out[:], ps_words[2][0:MID, 0:D], mid_x[:], ALU.add).then_inc(s_mres, 1)
            dve.wait_ge(s_slps, 1)
            v.tensor_copy(slow_n[:], ps_small[:, 0:1]).then_inc(s_sln, 1)

            dve.wait_ge(s_sln, 1)
            n_slow = dve.value_load(slow_n[0:1, 0:1], min_val=0, max_val=N)
            with dve.If(n_slow > 0):
                restart()
                step(v.memset(ranked, 0.0))
                dve.wait_ge(s_slin, 32)
                with dve.Fori(0, N) as r:
                    is_slow = dve.value_load(slow_row[0:1, bass.ds(r, 1)], min_val=0, max_val=1)
                    with dve.If(is_slow > 0):
                        restart()
                        dve.wait_ge(s_ra, 16)
                        dve.sem_clear(s_ra)
                        step(v.tensor_copy(x_col[:], xT[:, bass.ds(r, 1)]))
                        nb, rk_ = nbr[:, 0:N], rank[:, 0:N]
                        step(v.tensor_scalar(nb, a_row[:, 0:N], 0.0, None, ALU.not_equal))
                        step(v.tensor_tensor_scan(rk_, nb, nb, 0.0, ALU.add, ALU.bypass))
                        cnt = rank[:, N - 1:N]
                        step(v.tensor_copy(sci[:, 0:1], cnt))
                        step(v.tensor_scalar(sci[:, 1:2], sci[:, 0:1], 1, None, ALU.logical_shift_right))
                        step(v.tensor_copy(sc[:, 0:1], cnt))
                        step(v.tensor_tensor(sc[:, 1:2], sc[:, 0:1], sci[:, 1:2], ALU.subtract))
                        step(v.tensor_scalar(sc[:, 2:3], sc[:, 1:2], 2.0, None, ALU.mult))
                        step(v.tensor_scalar(sc[:, 3:4], sc[:, 0:1], 5.0, None, ALU.is_gt))
                        step(v.scalar_tensor_tensor(out=nb, in0=rk_, scalar=sc[:, 1:2], in1=nb, op0=ALU.not_equal,
                                                    op1=ALU.mult))
                        step(v.scalar_tensor_tensor(out=nb, in0=rk_, scalar=sc[:, 2:3], in1=nb, op0=ALU.not_equal,
                                                    op1=ALU.mult))
                        step(v.tensor_scalar(nb, nb, sc[:, 3:4], None, ALU.mult))
                        step(v.tensor_reduce(sc[:, 4:5], nb, AX.X, ALU.add))
                        step(v.tensor_tensor(vals[:, 0:N], xT, nb, ALU.mult))
                        step(v.tensor_scalar(nb, nb, -1.0, BIG, ALU.add, ALU.mult))
                        step(v.tensor_tensor(vals[:, 0:N], vals[:, 0:N], nb, ALU.add))
                        step(v.tensor_copy(sci[:, 2:3], sc[:, 4:5]))
                        step(v.memset(nbr, 1.0))
                        step(v.tensor_tensor_scan(rank, nbr, nbr, 0.0, ALU.add, ALU.bypass))
                        n_kept = dve.value_load(sci[0:1, 2:3], min_val=0, max_val=N)
                        with dve.Fori(0, NP // 8) as j:
                            with dve.If(n_kept > j * 8):
                                restart()
                                step(v.max(top8[:], vals[:, 0:N]))
                                step(v.tensor_copy(ranked[:, bass.ds(j * 8, 8)], top8[:]))
                                step(v.match_replace(vals[:, 0:N], top8[:], vals[:, 0:N], -BIG))
                        restart()
                        for q, (mul, add, shift) in enumerate(((1.0, 3.0, 2), (1.0, 1.0, 1), (3.0, 3.0, 2))):
                            step(v.tensor_scalar(sci[:, 3:4], sc[:, 4:5], mul, add, ALU.mult, ALU.add))
                            step(v.tensor_scalar(sci[:, 4:5], sci[:, 3:4], shift, None, ALU.logical_shift_right))
                            step(v.tensor_scalar(sc[:, 5:6], sci[:, 4:5], 1.0, None, ALU.max))
                            step(v.tensor_tensor(sc[:, 6:7], sc[:, 4:5], sc[:, 5:6], ALU.subtract))
                            step(v.tensor_scalar(sc[:, 7:8], sc[:, 6:7], 1.0, None, ALU.add))
                            step(v.scalar_tensor_tensor(out=nbr, in0=rank, scalar=sc[:, 7:8], in1=ranked,
                                                        op0=ALU.is_equal, op1=ALU.mult))
                            step(v.tensor_reduce(sc[:, 8 + q:9 + q], nbr, AX.X, ALU.add))
                        step(v.tensor_scalar(sc[:, 12:13], sc[:, 8:9], THIRD_HALF, None, ALU.mult))
                        step(v.scalar_tensor_tensor(out=sc[:, 13:14], in0=sc[:, 9:10], scalar=THIRD_HALF,
                                                    in1=sc[:, 12:13], op0=ALU.mult, op1=ALU.add))
                        step(v.scalar_tensor_tensor(out=sc[:, 14:15], in0=sc[:, 10:11], scalar=THIRD_HALF,
                                                    in1=sc[:, 13:14], op0=ALU.mult, op1=ALU.add))
                        v.scalar_tensor_tensor(out=comb_col[:], in0=x_col[:], scalar=0.5, in1=sc[:, 14:15],
                                               op0=ALU.mult, op1=ALU.add).then_inc(s_rc, 1)
                        dve.wait_ge(s_rp, 1)
                        dve.sem_clear(s_rp)
                        step(v.tensor_tensor(sc[:, 16:17], ps_out[0][:, 0:1], b_col[:], ALU.add))
                        v.tensor_tensor(out_col[:], sc[:, 16:17], x_col[:], ALU.add).then_inc(s_ro, 1)


_INS = ["x", "adj", "L0_gnn_W", "L0_gnn_b"]


def kernel(**inputs):
    import concourse.bacc as bacc
    from concourse.bass_utils import run_bass_kernel_spmd as run

    nc = bacc.Bacc("TRN2", target_bir_lowering=False, num_devices=1)
    arrays, args = {}, []
    for name in _INS:
        a = np.ascontiguousarray(inputs[name])
        arrays[f"in_{name}"] = a
        args.append(nc.dram_tensor(f"in_{name}", a.shape, mybir.dt.from_np(a.dtype), kind="ExternalInput").ap())
    rows, feats = arrays["in_x"].shape
    args.append(nc.dram_tensor("flag_rows", (rows,), I32, kind="Internal").ap())
    args.append(nc.dram_tensor("out_0", (rows, feats), F32, kind="ExternalOutput").ap())
    build(nc, *args)
    r = run(nc, [arrays], core_ids=[0])
    return r.results[0]["out_0"]
```
